# Optimizing a Trainium2 kernel written in Bass

```python
import numpy as np
import jax
import jax.numpy as jnp

def _softmax(x, axis=-1):
    return jax.nn.softmax(x, axis=axis)

def _gelu(x):
    return jax.nn.gelu(x, approximate=True)

def _silu(x):
    return jax.nn.silu(x)

def _sigmoid(x):
    return jax.nn.sigmoid(x)

def _layernorm(x, axis=-1, eps=1e-05):
    m = jnp.mean(x, axis=axis, keepdims=True)
    v = jnp.var(x, axis=axis, keepdims=True)
    return (x - m) / jnp.sqrt(v + eps)

def _scatter_add(tgt, idx, src, axis=0):
    return tgt.at[idx].add(src)

def _segment_sum(src, seg, n):
    return jax.ops.segment_sum(src, seg, n)
kernel_name = 'mk_gnn_preln_d4_gnn_r8_636a00'

def setup_inputs(seed: int=0):
    np.random.seed(seed)
    _w = jnp.asarray

    def _rec_inputs():
        import jax
        import jax.numpy as jnp
        _gk = jax.random.key(seed)
        x = -0.000202 + 1 * jax.random.normal(jax.random.fold_in(_gk, 1), (6250, 128), jnp.float32)
        _s = jax.random.randint(jax.random.fold_in(_gk, 2), (50000,), 0, 6250, jnp.int32)
        _d = jax.random.randint(jax.random.fold_in(_gk, 3), (50000,), 0, 6250, jnp.int32)
        _loop = jnp.arange(6250, dtype=jnp.int32)
        src = jnp.concatenate([_s, _d, _loop])
        dst = jnp.concatenate([_d, _s, _loop])
        _o = jnp.argsort(dst, stable=True)
        src = src[_o]
        dst = dst[_o]
        edge_attr3_4x1 = jax.random.uniform(jax.random.fold_in(_gk, 12), (106250, 4, 1), jnp.float32, 0.0, 1)
        edge_type_64 = jax.random.randint(jax.random.fold_in(_gk, 14), (106250,), 0, 64, jnp.int32)
        edge_weight1 = jax.random.uniform(jax.random.fold_in(_gk, 15), (106250, 1), jnp.float32, 0.0, 0.999998)
        return (x, src, dst, edge_attr3_4x1, edge_type_64, edge_weight1)
    x, src, dst, edge_attr3_4x1, edge_type_64, edge_weight1 = _rec_inputs()

    def _L0_gnn_setup():
        import jax, jax.numpy as jnp
        import numpy as np
        N_NODES = 6250
        N_EDGES = 100000
        D_IN = 128
        D_HID = 128

        def _sage_conv(h, src, dst, W_self, W_neigh, b):
            msg_sum = jax.ops.segment_sum(h[src], dst, num_segments=N_NODES)
            deg = jax.ops.segment_sum(jnp.ones_like(dst, dtype=h.dtype), dst, num_segments=N_NODES)
            h_neigh = msg_sum / jnp.maximum(deg, 1.0)[:, None]
            return h @ W_self + h_neigh @ W_neigh + b
        key = jax.random.key(seed)
        ks = jax.random.split(key, 10)
        inp = {'feats': jax.random.normal(ks[0], (N_NODES, D_IN), dtype=jnp.float32), 'src': jax.random.randint(ks[1], (N_EDGES,), 0, N_NODES, dtype=jnp.int32), 'dst': jax.random.randint(ks[2], (N_EDGES,), 0, N_NODES, dtype=jnp.int32)}
        dims = [(D_IN, D_HID), (D_HID, D_HID), (D_HID, D_HID)]
        for i, (di, do) in enumerate(dims):
            scale = 1.0 / np.sqrt(di)
            inp[f'W_self{i}'] = jax.random.normal(ks[3 + 2 * i], (di, do), dtype=jnp.float32) * scale
            inp[f'W_neigh{i}'] = jax.random.normal(ks[4 + 2 * i], (di, do), dtype=jnp.float32) * scale
            inp[f'b{i}'] = jnp.zeros((do,), dtype=jnp.float32)
        return inp
    _L0_gnn_all = _L0_gnn_setup()
    _L0_gnn_in = {k: v for k, v in _L0_gnn_all.items() if k in ('W_self0', 'W_neigh0', 'b0', 'W_self1', 'W_neigh1', 'b1', 'W_self2', 'W_neigh2', 'b2')}
    del _L0_gnn_all

    def _L1_gnn_setup():
        import jax, jax.numpy as jnp
        import numpy as np
        N = 6250
        E = 75000
        IN = 128
        H = 4
        C = 32
        B = 3
        NEG_SLOPE = 0.2
        key = jax.random.key(seed)
        ks = jax.random.split(key, 6)
        x = jax.random.normal(ks[0], (N, IN), dtype=jnp.float32)
        edge_index = jax.random.randint(ks[1], (2, E), 0, N)
        coeffs_t = jnp.array([0.25, 0.5, 0.25], dtype=jnp.float32)
        glorot_w = float(np.sqrt(2.0) * np.sqrt(6.0 / (H * C + IN)))
        glorot_a = float(np.sqrt(2.0) * np.sqrt(6.0 / (1 + C)))
        lin_weight = jax.random.uniform(ks[2], (B, H * C, IN), jnp.float32, -glorot_w, glorot_w)
        lin_bias = jnp.zeros((B, H * C), dtype=jnp.float32)
        att_src = jax.random.uniform(ks[3], (B, 1, H, C), jnp.float32, -glorot_a, glorot_a)
        att_dst = jax.random.uniform(ks[4], (B, 1, H, C), jnp.float32, -glorot_a, glorot_a)
        return {'x': x, 'edge_index': edge_index, 'coeffs_t': coeffs_t, 'lin_weight': lin_weight, 'lin_bias': lin_bias, 'att_src': att_src, 'att_dst': att_dst}
    _L1_gnn_all = _L1_gnn_setup()
    _L1_gnn_in = {k: v for k, v in _L1_gnn_all.items() if k in ('coeffs_t', 'lin_weight', 'lin_bias', 'att_src', 'att_dst')}
    del _L1_gnn_all

    def _L2_gnn_setup():
        import jax, jax.numpy as jnp
        import numpy as np
        N_NODES = 6250
        N_EDGES = 100000
        N_HEADS = 4
        FEAT = 128
        key = jax.random.key(seed)
        k1, k2, k3, k4 = jax.random.split(key, 4)
        h = jax.random.normal(k1, (N_NODES, FEAT), dtype=jnp.float32)
        e = jax.random.uniform(k2, (N_EDGES, N_HEADS, 1), dtype=jnp.float32)
        src = jax.random.randint(k3, (N_EDGES,), 0, N_NODES, dtype=jnp.int64)
        dst = jax.random.randint(k4, (N_EDGES,), 0, N_NODES, dtype=jnp.int64)
        return {'h': h, 'e': e, 'src': src, 'dst': dst}
    _L2_gnn_all = _L2_gnn_setup()
    _L2_gnn_in = {k: v for k, v in _L2_gnn_all.items() if k in ()}
    del _L2_gnn_all

    def _L3_gnn_setup():
        import jax, jax.numpy as jnp
        import numpy as np
        N, E, IN, OUT, R, B = (2500, 80000, 128, 128, 64, 16)
        key = jax.random.key(seed)
        ks = jax.random.split(key, 9)
        xav_w = float(np.sqrt(2.0 / (IN + OUT)))
        xav_c = float(np.sqrt(2.0 / (R + B)))
        return {'x': jax.random.normal(ks[0], (N, IN), jnp.float32), 'weight': jax.random.normal(ks[1], (B, IN, OUT), jnp.float32) * xav_w, 'w_comp': jax.random.normal(ks[2], (R, B), jnp.float32) * xav_c, 'h_bias': jnp.zeros((OUT,), jnp.float32), 'loop_weight': jax.random.normal(ks[3], (IN, OUT), jnp.float32) * xav_w, 'norm': jax.random.uniform(ks[4], (E, 1), jnp.float32), 'src': jax.random.randint(ks[5], (E,), 0, N, jnp.int32), 'dst': jax.random.randint(ks[6], (E,), 0, N, jnp.int32), 'etypes': jax.random.randint(ks[7], (E,), 0, R, jnp.int32)}
    _L3_gnn_all = _L3_gnn_setup()
    _L3_gnn_in = {k: v for k, v in _L3_gnn_all.items() if k in ('weight', 'w_comp', 'h_bias', 'loop_weight')}
    del _L3_gnn_all
    return {'x': x, 'src': src, 'dst': dst, 'edge_attr3_4x1': edge_attr3_4x1, 'edge_type_64': edge_type_64, 'edge_weight1': edge_weight1, 'L0_gnn_W_self0': _L0_gnn_in['W_self0'], 'L0_gnn_W_neigh0': _L0_gnn_in['W_neigh0'], 'L0_gnn_b0': _L0_gnn_in['b0'], 'L0_gnn_W_self1': _L0_gnn_in['W_self1'], 'L0_gnn_W_neigh1': _L0_gnn_in['W_neigh1'], 'L0_gnn_b1': _L0_gnn_in['b1'], 'L0_gnn_W_self2': _L0_gnn_in['W_self2'], 'L0_gnn_W_neigh2': _L0_gnn_in['W_neigh2'], 'L0_gnn_b2': _L0_gnn_in['b2'], 'L1_gnn_coeffs_t': _L1_gnn_in['coeffs_t'], 'L1_gnn_lin_weight': _L1_gnn_in['lin_weight'], 'L1_gnn_lin_bias': _L1_gnn_in['lin_bias'], 'L1_gnn_att_src': _L1_gnn_in['att_src'], 'L1_gnn_att_dst': _L1_gnn_in['att_dst'], 'L3_gnn_weight': _L3_gnn_in['weight'], 'L3_gnn_w_comp': _L3_gnn_in['w_comp'], 'L3_gnn_h_bias': _L3_gnn_in['h_bias'], 'L3_gnn_loop_weight': _L3_gnn_in['loop_weight']}

def reference(x, src, dst, edge_attr3_4x1, edge_type_64, edge_weight1, L0_gnn_W_self0, L0_gnn_W_neigh0, L0_gnn_b0, L0_gnn_W_self1, L0_gnn_W_neigh1, L0_gnn_b1, L0_gnn_W_self2, L0_gnn_W_neigh2, L0_gnn_b2, L1_gnn_coeffs_t, L1_gnn_lin_weight, L1_gnn_lin_bias, L1_gnn_att_src, L1_gnn_att_dst, L3_gnn_weight, L3_gnn_w_comp, L3_gnn_h_bias, L3_gnn_loop_weight):
    import jax
    import jax.numpy as jnp

    def _L0_gnn_ref(feats, src, dst, W_self0, W_neigh0, b0, W_self1, W_neigh1, b1, W_self2, W_neigh2, b2):
        import jax, jax.numpy as jnp
        import numpy as np
        N_NODES = 6250
        N_EDGES = 100000
        D_IN = 128
        D_HID = 128

        def _sage_conv(h, src, dst, W_self, W_neigh, b):
            msg_sum = jax.ops.segment_sum(h[src], dst, num_segments=N_NODES)
            deg = jax.ops.segment_sum(jnp.ones_like(dst, dtype=h.dtype), dst, num_segments=N_NODES)
            h_neigh = msg_sum / jnp.maximum(deg, 1.0)[:, None]
            return h @ W_self + h_neigh @ W_neigh + b
        layers = [(W_self0, W_neigh0, b0), (W_self1, W_neigh1, b1), (W_self2, W_neigh2, b2)]
        h = feats
        last = len(layers) - 1
        for i, (ws, wn, b) in enumerate(layers):
            h = _sage_conv(h, src, dst, ws, wn, b)
            if i != last:
                h = jax.nn.relu(h)
        return h

    def _L1_gnn_ref(x, edge_index, coeffs_t, lin_weight, lin_bias, att_src, att_dst):
        import jax, jax.numpy as jnp
        import numpy as np
        N = 6250
        E = 75000
        IN = 128
        H = 4
        C = 32
        B = 3
        NEG_SLOPE = 0.2
        W = jnp.einsum('b,boi->oi', coeffs_t, lin_weight)
        bias = jnp.einsum('b,bo->o', coeffs_t, lin_bias)
        a_src = jnp.einsum('b,bqhc->qhc', coeffs_t, att_src)
        a_dst = jnp.einsum('b,bqhc->qhc', coeffs_t, att_dst)
        n = x.shape[0]
        xt = (x @ W.T + bias).reshape(n, H, C)
        alpha_src = jnp.sum(xt * a_src, axis=-1)
        alpha_dst = jnp.sum(xt * a_dst, axis=-1)
        row, col = (edge_index[0], edge_index[1])
        alpha = alpha_src[row] + alpha_dst[col]
        alpha = jax.nn.leaky_relu(alpha, NEG_SLOPE)
        amax = jax.ops.segment_max(alpha, col, num_segments=n)
        ex = jnp.exp(alpha - amax[col])
        denom = jax.ops.segment_sum(ex, col, num_segments=n)
        alpha = ex / (denom[col] + 1e-16)
        msg = xt[row] * alpha[..., None]
        out = jax.ops.segment_sum(msg, col, num_segments=n)
        return out.reshape(n, H * C)

    def _L2_gnn_ref(h, e, src, dst):
        import jax, jax.numpy as jnp
        import numpy as np
        N_NODES = 6250
        N_EDGES = 100000
        N_HEADS = 4
        FEAT = 128
        N = h.shape[0]
        H = e.shape[-2]
        x = h.reshape(N, H, -1)
        src2 = jnp.concatenate([src, dst])
        dst2 = jnp.concatenate([dst, src])
        e2 = jnp.concatenate([e, e], axis=0)
        e_sum = jax.ops.segment_sum(e2, dst2, num_segments=N)
        e2 = e2 / e_sum[dst2]
        gamma = 0.0
        loop = jnp.arange(N, dtype=src.dtype)
        src3 = jnp.concatenate([src2, loop])
        dst3 = jnp.concatenate([dst2, loop])
        e3 = jnp.concatenate([e2, jnp.full((N, H, 1), gamma, dtype=e.dtype)], axis=0)
        e3 = jnp.where((src3 == dst3)[:, None, None], gamma, e3)

        def f(y):
            return jax.ops.segment_sum(y[src3] * e3, dst3, num_segments=N)
        dt = jnp.asarray(1.0, dtype=h.dtype)
        k1 = f(x)
        k2 = f(x + dt * k1 / 3)
        k3 = f(x + dt * (k2 - k1 / 3))
        k4 = f(x + dt * (k1 - k2 + k3))
        y = x + dt * 0.125 * (k1 + 3 * (k2 + k3) + k4)
        return y.reshape(N, -1)

    def _L3_gnn_ref(x, weight, w_comp, h_bias, loop_weight, norm, src, dst, etypes):
        import jax, jax.numpy as jnp
        import numpy as np
        N, E, IN, OUT, R, B = (2500, 80000, 128, 128, 64, 16)
        W_rel = jnp.einsum('rb,bio->rio', w_comp, weight)
        h_all = jnp.einsum('ni,rio->nro', x, W_rel)
        msg = h_all[src, etypes] * norm
        agg = jax.ops.segment_sum(msg, dst, num_segments=x.shape[0])
        out = agg + h_bias + x @ loop_weight
        return jax.nn.relu(out)
    edge_index = jnp.stack([src, dst])
    h = jnp.maximum(_layernorm(x, axis=-1), 0.0)
    x = x + _L0_gnn_ref(h, src, dst, L0_gnn_W_self0, L0_gnn_W_neigh0, L0_gnn_b0, L0_gnn_W_self1, L0_gnn_W_neigh1, L0_gnn_b1, L0_gnn_W_self2, L0_gnn_W_neigh2, L0_gnn_b2)
    h = jnp.maximum(_layernorm(x, axis=-1), 0.0)
    x = x + _L1_gnn_ref(h, edge_index, L1_gnn_coeffs_t, L1_gnn_lin_weight, L1_gnn_lin_bias, L1_gnn_att_src, L1_gnn_att_dst)
    h = jnp.maximum(_layernorm(x, axis=-1), 0.0)
    x = x + _L2_gnn_ref(h, edge_attr3_4x1, src, dst)
    h = jnp.maximum(_layernorm(x, axis=-1), 0.0)
    x = x + _L3_gnn_ref(h, L3_gnn_weight, L3_gnn_w_comp, L3_gnn_h_bias, L3_gnn_loop_weight, edge_weight1, src, dst, edge_type_64)
    return x

_drawn_inputs = setup_inputs


def setup_inputs(seed=0):
    import zlib

    import numpy as np

    out = dict(_drawn_inputs(seed))
    spreads = {'L0_gnn_b0': (0.0, 0.1),
     'L0_gnn_b1': (0.0, 0.1),
     'L0_gnn_b2': (0.0, 0.1),
     'L1_gnn_lin_bias': (0.0, 0.1),
     'L3_gnn_h_bias': (0.0, 0.337)}
    factors = {'L1_gnn_att_dst': 5.1}
    for name, (base, spread) in spreads.items():
        noise = np.random.default_rng([zlib.crc32(name.encode()), seed]).standard_normal(out[name].shape)
        drawn = base * np.exp(spread * noise) if base else spread * noise
        out[name] = jnp.asarray(drawn.astype(out[name].dtype))
    for name, factor in factors.items():
        out[name] = (out[name] * factor).astype(out[name].dtype)
    return out
```

```python
from contextlib import ExitStack

import concourse.bass as bass
from concourse import mybir

F32 = mybir.dt.float32
BF16 = mybir.dt.bfloat16
I32 = mybir.dt.int32
ALU = mybir.AluOpType
ACT = mybir.ActivationFunctionType
AX = mybir.AxisListType.X

P = 128
NODES = 6250
FEAT = 128
HEADS = 4
HC = FEAT // HEADS
EDGES = 106250
RELS = 64
BASES = 16
COEFS = 3
BLOCKS = -(-NODES // P)
LAST = NODES - (BLOCKS - 1) * P
ROWS = BLOCKS * P

EP = 125
EC = EDGES // EP
CT = 10
CHUNKS = EC // CT
CU = 5
CI = CHUNKS // CU
CB = CT * BLOCKS
SU = 10
SI = EC // SU

UNROLL = 16
HALF = UNROLL // 2
MAX_TILES = (EDGES + BLOCKS * (P - 1)) // P
TILES = -(-MAX_TILES // UNROLL) * UNROLL
ITERS = TILES // UNROLL
RING = 4
W = 8
AUX = FEAT + HEADS

GB = 7
GI = BLOCKS // GB
BIG = float(2.0 ** 100)
TINY = float(2.0 ** -126)
LN_EPS = 1e-5
SLOPE = 0.2
assert EP * EC == EDGES and CI * CU * CT == EC and SI * SU == EC and GB * GI == BLOCKS
assert TILES % 8 == 0 and TILES // 8 <= P and CB <= 512

PASSES = ["sage0 F", "sage1 F", "sage2 F", "peak F", "share F", "gat F",
          "rk0 F", "rk0 R", "rk1 F", "rk1 R", "rk2 F", "rk2 R", "rk3 F", "rk3 R", "rel F"]
GATHERED = [p for p in PASSES if p != "share F"]
ACCUMULATED = [p for p in PASSES if p not in ("share F",)]
WEIGHTED = [p for p in PASSES if p[:3] in ("gat", "rk0", "rk1", "rk2", "rk3")]
TABLES = ["sage0", "sage1", "sage2", "gat", "rk0", "rk1", "rk2", "rk3"]


PAUSES = {"sage0 F": 12, "sage1 F": 12, "sage2 F": 24, "peak F": 29, "gat F": 8}


def gnn_kernel(nc, x, src, dst, edge_attr, edge_type, edge_weight, W_self0, W_neigh0, b0, W_self1,
               W_neigh1, b1, W_self2, W_neigh2, b2, coeffs, lin_weight, lin_bias, att_src, att_dst,
               rel_weight, w_comp, h_bias, loop_weight, out):
    with ExitStack() as ctx:
        def sb(name, shape, dt=F32):
            return ctx.enter_context(nc.sbuf_tensor(name, shape, dt))

        def sem(name):
            return ctx.enter_context(nc.semaphore(name))

        def dram(name, shape, dt=F32):
            return nc.dram_tensor(name, shape, dt, kind="Internal").ap()

        ctx.enter_context(nc.allow_non_contiguous_dma("rows of single words"))

        table = dram("table", (ROWS, FEAT))
        peak_table = dram("peak_table", (ROWS, HEADS))
        rel_table = dram("rel_table", (ROWS * RELS, FEAT))
        list_dram = {"F": dram("list_f", (P * TILES, W)), "R": dram("list_r", (P * TILES, W))}
        block_dram = {"F": dram("block_f", (TILES,), I32), "R": dram("block_r", (TILES,), I32)}

        X = sb("X", [P, BLOCKS, FEAT])
        H = sb("H", [P, BLOCKS, FEAT])
        work = sb("work", [P, BLOCKS * (FEAT + AUX)])
        K = work[:, 0:BLOCKS * FEAT].rearrange("p (b f) -> p b f", f=FEAT)
        ACC = work[:, BLOCKS * FEAT:].rearrange("p (b f) -> p b f", f=AUX)
        lists = {"F": sb("list_F", [P, TILES, W]), "R": sb("list_R", [P, TILES, W])}
        other = {"F": sb("other_F", [P, TILES]), "R": sb("other_R", [P, TILES])}
        block_of = {"F": sb("block_F", [1, TILES], I32), "R": sb("block_R", [1, TILES], I32)}
        rows = sb("rows", [P, UNROLL, AUX])
        scaled = sb("scaled", [P, RING, AUX])
        onehot = sb("onehot", [P, RING, P])
        index = sb("index", [P, UNROLL], I32)
        record = sb("record", [EP, SU, W])
        target = sb("target", [EP, SU], I32)
        share16 = sb("share16", [P, UNROLL, HEADS])
        iota_i = sb("iota_i", [P, P], I32)
        part_i = sb("part_i", [P, 1], I32)
        iota = sb("iota", [P, P])
        iota_bf = sb("iota_bf", [P, P], BF16)
        part = sb("part", [P, 1])
        ident = sb("ident", [P, P])
        earlier = sb("earlier", [P, P], BF16)
        ones = sb("ones", [P, P], BF16)
        zeros = sb("zeros", [P, 512], BF16)
        w_pair = sb("w_pair", [P, 6, FEAT])
        bias = sb("bias", [P, 5, FEAT])
        a_src = sb("a_src", [P, FEAT])
        a_dst = sb("a_dst", [P, FEAT])
        coef = sb("coef", [P, COEFS])
        w_gat = sb("w_gat", [P, FEAT])
        w_loop = sb("w_loop", [P, FEAT])
        w_comp_t = sb("w_comp_t", [BASES, RELS])
        stat = sb("stat", [P, 4, BLOCKS])
        rdeg = sb("rdeg", [P, BLOCKS])
        PEAK = sb("PEAK", [P, BLOCKS, HEADS])
        ADM = sb("ADM", [P, BLOCKS, 2 * HEADS])
        REC = sb("REC", [P, BLOCKS, HEADS])
        peak_tile = sb("peak_tile", [P, HEADS])
        turned_a = sb("turned_a", [P, GB, P])
        turned_b = sb("turned_b", [P, GB, P])
        mean = sb("mean", [P, GB, P])
        held = rows[:, :, :].rearrange("p s f -> p (s f)")[:, 0:GB * P].rearrange("p (g f) -> p g f", f=P)
        share = work[:, 0:TILES * HEADS].rearrange("p (t h) -> p t h", h=HEADS)
        scratch = work[:, BLOCKS * FEAT:]
        diag = scratch[:, 0:RING * HEADS * P].rearrange("p (s h e) -> p s h e", s=RING, h=HEADS)
        absent = scratch[:, 2048:2048 + RING * P // 2].bitcast(BF16).rearrange("p (s e) -> p s e", s=RING)
        never = scratch[:, 2304:2304 + P // 2].bitcast(BF16)
        adm16 = scratch[:, 3200:3200 + UNROLL * 2 * HEADS].rearrange("p (t h) -> p t h", h=2 * HEADS)
        alpha16 = scratch[:, 3400:3400 + 2 * UNROLL * HEADS].rearrange("p (s t h) -> p s t h", s=2, h=HEADS)
        hflat = H[:, :, :].rearrange("p b f -> p (b f)")
        onehot4 = hflat[:, 0:2 * RING * P].rearrange("p (s t e) -> p s t e", s=2, t=RING)
        member4 = hflat[:, 2 * RING * P:4 * RING * P].rearrange("p (s t e) -> p s t e", s=2, t=RING)
        W_REL = work[:, 0:RELS * FEAT]
        SQ = 4 * 512
        stage = lists["R"][:, :, :].rearrange("p t w -> p (t w)")[:, 0:3 * SQ].rearrange("p (s n) -> p s n", s=3)
        bases_sb = work[0:BASES, RELS * FEAT:RELS * FEAT + 4096].rearrange("b (i o) -> b i o", o=32)

        def place(at, n, dt=F32, p=EP):
            v = work[0:p, at:at + n]
            return v if dt == F32 else v.bitcast(dt)

        src_i, dst_i, type_i = (place(EC * k, EC, I32) for k in range(3))
        norm_f = place(EC * 3, EC)
        attr_f = place(EC * 4, EC * HEADS)
        hi_f = {"F": place(EC * 8, EC), "R": place(EC * 9, EC)}
        key_t = place(EC * 10, EC, I32)
        pos_f = place(EC * 11, EC)
        self_f = place(EC * 12, EC)
        to_row = {"F": place(0, EC, I32), "R": other["R"][0:EP, 0:EC].bitcast(I32)}
        member_bf = work[0:EP, 900:900 + CU * CB // 2].bitcast(BF16).rearrange("p (s n) -> p s n", s=CU)
        rank_t = work[0:EP, 2200:2200 + CB]
        carry = work[:, 2700:2700 + BLOCKS]
        small = work[:, 2750:2750 + 5 * BLOCKS].rearrange("p (k b) -> p k b", k=5)
        small_i = work[:, 3150:3150 + BLOCKS].bitcast(I32)
        tile_no_i = work[:, 11060:11068].bitcast(I32)
        tile_no = work[:, 11068:11076]
        tile_blk = work[:, 11076:11084]
        tile_blk_i = work[:, 11084:11092].bitcast(I32)
        tile_cmp = work[:, 11100:11100 + 8 * BLOCKS].rearrange("p (t b) -> p t b", b=BLOCKS)

        ps = ctx.enter_context(nc.psum_tensor("ps", [P, 8, 512], F32))

        raw_loaded = sem("raw_loaded")
        weights_loaded = sem("weights_loaded")
        x_loaded = sem("x_loaded")
        iotas = sem("iotas")
        consts = sem("consts")
        pads_ready = sem("pads_ready")
        pads_written = sem("pads_written")
        chunk_members = sem("chunk_members")
        chunk_summed = sem("chunk_summed")
        chunk_ranked = sem("chunk_ranked")
        counts_closed = sem("counts_closed")
        blocks_ready = sem("blocks_ready")
        blocks_written = sem("blocks_written")
        blocks_loaded = sem("blocks_loaded")
        records_ready = sem("records_ready")
        staged = sem("staged")
        scattered = [sem(f"scattered{s}") for s in range(SU)]
        list_loaded = sem("list_loaded")
        step = sem("step")
        table_ready = sem("table_ready")
        table_written = sem("table_written")
        variance = sem("variance")
        root = sem("root")
        index_ready = sem("index_ready")
        landed = [sem(f"landed{s}") for s in range(UNROLL)]
        tile_members = sem("tile_members")
        tile_scaled = sem("tile_scaled")
        summed = sem("summed")
        added = sem("added")
        diag_ready = sem("diag_ready")
        turned = sem("turned")
        turned_copied = sem("turned_copied")
        fetched = sem("fetched")
        fetch_read = sem("fetch_read")
        shares_raw = sem("shares_raw")
        shares_exp = sem("shares_exp")
        dense_in = sem("dense_in")
        dense_turned = sem("dense_turned")
        dense_copied = sem("dense_copied")
        dense_out = sem("dense_out")
        gat_mixed = sem("gat_mixed")
        gat_turned = sem("gat_turned")
        layer_ready = sem("layer_ready")
        bases_loaded = sem("bases_loaded")
        bases_free = sem("bases_free")
        rel_mixed = sem("rel_mixed")
        rel_copied = sem("rel_copied")
        rel_product = sem("rel_product")
        rel_staged = sem("rel_staged")
        block_held = sem("block_held")
        rel_written = [sem(f"rel_written{s}") for s in range(3)]
        peak_consts = sem("peak_consts")
        go = sem("go")
        result_ready = sem("result_ready")
        written = sem("written")

        def tiles_before(which, name):
            return TILES * which.index(name)

        def table_at(eng, name):
            eng.wait_ge(table_written, 16 * (TABLES.index(name) + 1 + (TABLES.index(name) >= 3)))

        def blocks_of_body(engine, key, i):
            _, values = nc.values_load_multi_w_load_instructions(
                block_of[key][0:1, bass.ds(i * UNROLL, UNROLL)], engines=(engine,), min_val=0, max_val=BLOCKS - 1,
                skip_runtime_bounds_check_because="each is a count of BLOCKS - 1 comparisons")
            return values

        block = ctx.enter_context(nc.Block())

        @block.sync
        def _(sp):
            for view, arr in ((src_i, src), (dst_i, dst), (type_i, edge_type)):
                sp.dma_start(view, arr.rearrange("(p c) -> p c", p=EP)).then_inc(raw_loaded, 16)
            sp.dma_start(norm_f, edge_weight.rearrange("(p c) o -> p (c o)", p=EP)).then_inc(raw_loaded, 16)
            sp.dma_start(attr_f, edge_attr.rearrange("(p c) h o -> p (c h o)", p=EP)).then_inc(raw_loaded, 16)
            sp.wait_ge(pads_ready, 2)
            for key in "FR":
                sp.dma_start(list_dram[key].rearrange("(p t) w -> p (t w)", p=P),
                             lists[key][:, :, :].rearrange("p t w -> p (t w)")).then_inc(pads_written, 16)
            sp.dma_start(X[:, 0:BLOCKS - 1, :], x[0:(BLOCKS - 1) * P, :].rearrange("(b p) f -> p b f", p=P)).then_inc(x_loaded, 16)
            sp.dma_start(X[0:LAST, BLOCKS - 1, :], x[(BLOCKS - 1) * P:NODES, :]).then_inc(x_loaded, 16)
            for k, key in enumerate("FR"):
                sp.wait_ge(blocks_ready, k + 1)
                sp.dma_start(block_dram[key].rearrange("(p j) -> p j", j=8), tile_blk_i[0:TILES // 8, :]).then_inc(blocks_written, 16)
                sp.wait_ge(blocks_written, 16 * (k + 1))
                sp.dma_start(block_of[key][:, :], block_dram[key].rearrange("(o t) -> o t", o=1)).then_inc(blocks_loaded, 16)
            def load_list(k, key):
                for q in range(SU):
                    sp.wait_ge(scattered[q], 16 * SI * (k + 1))
                sp.dma_start(lists[key][:, :, :].rearrange("p t w -> p (t w)"),
                             list_dram[key].rearrange("(p t) w -> p (t w)", p=P)).then_inc(list_loaded, 16)

            n = 0
            for name in TABLES:
                sp.wait_ge(table_ready, n + 1)
                rows_of = ACC[:, :, 0:FEAT] if name in ("rk1", "rk2", "rk3") else H[:, :, :]
                sp.dma_start(table.rearrange("(b p) f -> p b f", p=P), rows_of).then_inc(table_written, 16)
                n += 1
                if name == "gat":
                    sp.wait_ge(table_ready, n + 1)
                    sp.dma_start(peak_table.rearrange("(b p) h -> p b h", p=P), PEAK[:, :, :]).then_inc(table_written, 16)
                    n += 1
                if name == "sage0":
                    load_list(0, "F")
                if name == "rk0":
                    load_list(1, "R")
            for q in range(4):
                if q == 0:
                    sp.wait_ge(bases_free, 1)
                else:
                    sp.wait_ge(rel_copied, 4 * q)
                sp.dma_start(bases_sb, rel_weight[:, :, q * 32:(q + 1) * 32]).then_inc(bases_loaded, 16)
            rel_rows = rel_table.rearrange("(b p r) f -> p b (r f)", p=P, r=RELS)
            for q in range(4):
                if q < 3:
                    sp.wait_ge(rel_staged, q + 1)
                    sp.dma_start(rel_rows[:, 0, q * SQ:(q + 1) * SQ], stage[:, q, :]).then_inc(rel_written[q], 16)
            sp.wait_ge(rel_staged, 4)
            sp.dma_start(rel_rows[:, 0, 3 * SQ:], stage[:, 0, :]).then_inc(rel_written[0], 16)
            with sp.Fori(0, (BLOCKS - 1) // 3) as i:
                for n in range(12):
                    sp.wait_ge(rel_staged, i * 12 + (5 + n))
                    sp.dma_start(rel_rows[:, bass.ds(i * 3 + (1 + n // 4), 1), (n % 4) * SQ:(n % 4 + 1) * SQ],
                                 stage[:, (n + 1) % 3, :]).then_inc(rel_written[(n + 1) % 3], 16)
            sp.wait_ge(result_ready, 1)
            sp.dma_start(out[0:(BLOCKS - 1) * P, :].rearrange("(b p) f -> p b f", p=P), X[:, 0:BLOCKS - 1, :]).then_inc(written, 16)
            sp.dma_start(out[(BLOCKS - 1) * P:NODES, :], X[0:LAST, BLOCKS - 1, :]).then_inc(written, 16)
            sp.wait_ge(written, 32)

        @block.gpsimd
        def _(pool):
            nc.gpsimd.iota(iota_i[:, :], pattern=[[1, P]], base=0, channel_multiplier=0).then_inc(iotas, 1)
            nc.gpsimd.iota(part_i[:, :], pattern=[[0, 1]], base=0, channel_multiplier=1).then_inc(iotas, 1)
            nc.gpsimd.iota(tile_no_i, pattern=[[1, 8]], base=0, channel_multiplier=8).then_inc(iotas, 1)
            def scatters(k, key, i, first=False):
                half = SU // 2
                for h in range(2):
                    a = h * half
                    if not first:
                        for q in range(a, a + half):
                            pool.wait_ge(scattered[q], i * 16 + 16 * SI * k)
                            pool.sem_inc(go, 1)
                    c = slice(a, a + half) if first else bass.ds(i * SU + a, half)
                    nc.gpsimd.tensor_copy(target[:, a:a + half], to_row[key][:, c]).then_inc(staged, 1)
                    nc.gpsimd.tensor_copy(record[:, a:a + half, :], lists[key][0:EP, c, :]).then_inc(staged, 1)
                    pool.wait_ge(staged, 2 * h + 2 if first else i * 4 + (4 * SI * k + 2 * h + 2))
                    if not first:
                        pool.sem_inc(go, 1)
                    for q in range(a, a + half):
                        pool.indirect_dma_start(out=list_dram[key], out_offset=bass.IndirectOffsetOnAxis(ap=target[:, q:q + 1], axis=0),
                                                in_=record[:, q, :], in_offset=None).then_inc(scattered[q], 16)

            pool.wait_ge(pads_written, 32)
            pool.wait_ge(records_ready, 1)
            scatters(0, "F", 0, first=True)
            with pool.Fori(1, SI) as i:
                scatters(0, "F", i)

            def gathers(name, from_table, columns):
                n0 = tiles_before(GATHERED, name)
                m0 = tiles_before(PASSES, name)
                with pool.Fori(0, ITERS) as i:
                    for s in range(UNROLL):
                        if s % HALF == 0:
                            pool.wait_ge(index_ready, i * 2 + (n0 // HALF + s // HALF + 1))
                            pool.sem_inc(go, 1)
                        pool.wait_ge(summed, i * UNROLL + (m0 + s + 1))
                        pool.sem_inc(go, 1)
                        pool.indirect_dma_start(out=rows[:, s, 0:columns], out_offset=None, in_=from_table,
                                                in_offset=bass.IndirectOffsetOnAxis(ap=index[:, s:s + 1], axis=0)).then_inc(landed[s], 16)

            done = 0
            for name in GATHERED:
                stage_name = name.split()[0]
                if stage_name in TABLES:
                    table_at(pool, stage_name)
                    gathers(name, table, FEAT)
                elif stage_name == "peak":
                    pool.wait_ge(table_written, 16 * 5)
                    gathers(name, peak_table, HEADS)
                else:
                    for s in range(3):
                        pool.wait_ge(rel_written[s], 16 * len([n for n in range(4 * BLOCKS) if n % 3 == s]))
                    gathers(name, rel_table, FEAT)
                if name in PAUSES:
                    pool.wait_ge(records_ready, 2)
                    with pool.Fori(done, done + PAUSES[name]) as i:
                        scatters(1, "R", i)
                    done += PAUSES[name]
            assert done == SI

        @block.scalar
        def _(act):
            loads = [(w_pair[:, n, :], w) for n, w in enumerate((W_self0, W_neigh0, W_self1, W_neigh1, W_self2, W_neigh2))]
            loads += [(w_loop[:, :], loop_weight), (w_comp_t[:, :], w_comp.rearrange("r b -> b r")),
                      (coef[:, :], coeffs.partition_broadcast(P)), (bias[:, 4, :], h_bias.partition_broadcast(P))]
            loads += [(bias[:, n, :], b.partition_broadcast(P)) for n, b in enumerate((b0, b1, b2))]
            loads += [(turned_a[:, 0:COEFS, :], lin_weight.rearrange("b o i -> o b i")),
                      (turned_a[:, 3:3 + COEFS, :], lin_bias.rearrange("b o -> (b o)").partition_broadcast(P)),
                      (turned_b[:, 0:COEFS, :], att_src.rearrange("b q h c -> (b q h c)").partition_broadcast(P)),
                      (turned_b[:, 3:3 + COEFS, :], att_dst.rearrange("b q h c -> (b q h c)").partition_broadcast(P))]
            for view, arr in loads:
                act.dma_start(view, arr).then_inc(weights_loaded, 16)

            act.sem_inc(shares_exp, 1)
            def indices(name):
                n0 = tiles_before(PASSES, name)
                word = 1 if name == "rel F" else 0
                key = name[-1]
                with act.Fori(0, ITERS) as i:
                    for h in range(2):
                        act.wait_ge(summed, i * UNROLL + (n0 + (h + 1) * HALF))
                        act.sem_inc(go, 1)
                        nc.scalar.copy(index[:, h * HALF:(h + 1) * HALF],
                                       lists[key][:, bass.ds(i * UNROLL + h * HALF, HALF), word]).then_inc(index_ready, 1)

            def root_of(k):
                act.wait_ge(variance, k + 1)
                nc.scalar.sqrt(stat[:, 2, :], stat[:, 1, :]).then_inc(root, 1)

            def peak_pass():
                n0, g0 = tiles_before(PASSES, "peak F"), tiles_before(GATHERED, "peak F")

                def refill(i_from, h):
                    act.wait_ge(summed, i_from * UNROLL + (n0 + UNROLL + (h + 1) * HALF))
                    act.sem_inc(go, 1)
                    nc.scalar.copy(index[:, h * HALF:(h + 1) * HALF],
                                   lists["F"][:, bass.ds(i_from * UNROLL + UNROLL + h * HALF, HALF), 0]).then_inc(index_ready, 1)

                def diagonals(i, s):
                    act.wait_ge(landed[s], i * 16 + (g0 + 16))
                    act.sem_inc(go, 1)
                    act.wait_ge(summed, i * UNROLL + (n0 + s + UNROLL - RING + 1))
                    act.sem_inc(go, 1)
                    for h in range(HEADS - 1):
                        nc.scalar.mul(diag[:, s % RING, h, :], ident[:, :], rows[:, s, h:h + 1]).then_inc(diag_ready, 1)

                for h in range(2):
                    act.wait_ge(summed, n0 + (h + 1) * HALF)
                    nc.scalar.copy(index[:, h * HALF:(h + 1) * HALF],
                                   lists["F"][:, h * HALF:(h + 1) * HALF, 0]).then_inc(index_ready, 1)
                with act.Fori(0, ITERS - 1) as i:
                    for s in range(UNROLL):
                        diagonals(i, s)
                        if s == HALF + 1:
                            refill(i, 0)
                    refill(i, 1)
                for s in range(UNROLL):
                    diagonals(ITERS - 1, s)

            def share_pass():
                n0 = tiles_before(PASSES, "share F")
                with act.Fori(0, ITERS) as i:
                    for g in range(UNROLL // RING):
                        act.wait_ge(turned, i * (UNROLL // RING) + (g + 3))
                        nc.scalar.copy(member4[:, g % 2, :, :].rearrange("p t e -> p (t e)"), ps[:, 4 + g % 2, :]).then_inc(turned_copied, 1)
                    act.wait_ge(shares_raw, i + 1)
                    act.sem_inc(go, 1)
                    at = share[:, bass.ds(i * UNROLL, UNROLL), :]
                    nc.scalar.activation(at, alpha16[:, 1, :, :], ACT.Exp).then_inc(shares_exp, 1)

            root_of(0)
            act.wait_ge(list_loaded, 16)
            for name in PASSES:
                if name == "peak F":
                    root_of(1)
                    act.wait_ge(peak_consts, 1)
                    peak_pass()
                elif name == "share F":
                    share_pass()
                else:
                    if name == "rk0 F":
                        root_of(2)
                    if name == "rel F":
                        root_of(3)
                    if name == "rk0 R":
                        act.wait_ge(list_loaded, 32)
                    indices(name)

        class Steps:

            def __init__(self, dve):
                self.dve, self.n, self.reg, self.per = dve, 0, None, 0

            def __call__(self, ins, wait=True):
                self.n += 1
                ins.then_inc(step, 1)
                if wait:
                    self.dve.wait_ge(step, self.n if self.reg is None else self.reg * self.per + self.n)

            def enter(self, reg, per):
                self.reg, self.per, self.n0 = reg, per, self.n

            def leave(self, trips):
                assert self.n - self.n0 == self.per, (self.n - self.n0, self.per)
                self.n = self.n0 + self.per * trips
                self.reg = None

        @block.vector
        def _(dve):
            v = nc.vector

            def move(into, of):
                return v.tensor_scalar(into, of, 1.0, None, ALU.mult)

            st = Steps(dve)
            dve.sem_inc(chunk_ranked, 2)
            dve.sem_inc(added, RING)
            dve.sem_inc(fetch_read, 1)

            dve.wait_ge(iotas, 3)
            st(v.tensor_copy(iota[:, :], iota_i[:, :]), False)
            st(v.tensor_copy(iota_bf[:, :], iota_i[:, :]), False)
            st(v.tensor_copy(part[:, :], part_i[:, :]), False)
            st(v.tensor_copy(tile_no, tile_no_i))
            v.tensor_scalar(ident[:, :], iota[:, :], part[:, 0:1], None, ALU.is_equal).then_inc(consts, 1)
            v.tensor_scalar(earlier[:, :], iota[:, :], part[:, 0:1], None, ALU.is_gt).then_inc(consts, 1)
            v.memset(ones[:, :], 1.0).then_inc(consts, 1)
            v.memset(zeros[:, :], 0.0).then_inc(consts, 1)
            st(v.memset(rows[:, :, :], 1.0), False)
            st(v.memset(X[:, BLOCKS - 1, :], 0.0), False)
            for key in "FR":
                st(v.memset(lists[key][:, :, :], 0.0))
                v.memset(lists[key][:, :, 2], -1.0).then_inc(pads_ready, 1)

            dve.wait_ge(raw_loaded, 80)
            dve.wait_ge(pads_written, 32)
            st(v.tensor_tensor(self_f, src_i, dst_i, ALU.is_equal))
            for key, near, far in (("F", dst_i, src_i), ("R", src_i, dst_i)):
                rec = lists[key][0:EP, 0:EC, :]
                st(v.tensor_scalar(key_t, near, 7, None, ALU.arith_shift_right))
                st(v.tensor_copy(hi_f[key], key_t))
                st(v.tensor_scalar(key_t, near, P - 1, None, ALU.bitwise_and))
                st(v.scalar_tensor_tensor(out=rec[:, :, 2], in0=self_f, scalar=float(P), in1=key_t, op0=ALU.mult, op1=ALU.add))
                st(v.tensor_copy(rec[:, :, 0], far))
                st(v.tensor_copy(rec[:, :, 3:3 + HEADS], attr_f.rearrange("p (c h) -> p c h", h=HEADS)))
            rec = lists["F"][0:EP, 0:EC, :]
            st(v.scalar_tensor_tensor(out=rec[:, :, 1], in0=src_i, scalar=float(RELS), in1=type_i, op0=ALU.mult, op1=ALU.add))
            st(v.tensor_copy(rec[:, :, 7], norm_f))

            def members(key, i, t, m0):
                dve.wait_ge(chunk_summed, i * CU + (m0 + t + 1))
                hi = hi_f[key][:, bass.ds(i * CU * CT + t * CT, CT)].unsqueeze(2).to_broadcast([EP, CT, BLOCKS])
                v.tensor_tensor(member_bf[:, t, :].rearrange("p (c b) -> p c b", b=BLOCKS), hi,
                                iota[0:EP, 0:BLOCKS].unsqueeze(1).to_broadcast([EP, CT, BLOCKS]),
                                ALU.is_equal).then_inc(chunk_members, 1)

            for k, key in enumerate("FR"):
                m0 = 2 * k * CHUNKS
                with dve.Fori(0, CI) as i:
                    for t in range(CU):
                        members(key, i, t, m0)
                dve.wait_ge(counts_closed, k + 1)
                st(v.tensor_reduce(small[:, 0, :], ps[:, 6, 0:CB].rearrange("p (c b) -> p b c", b=BLOCKS), AX, ALU.add))
                st(v.tensor_scalar(small_i, small[:, 0, :], float(P - 1), None, ALU.add))
                st(v.tensor_scalar(small_i, small_i, 7, None, ALU.arith_shift_right))
                st(v.tensor_copy(small[:, 1, :], small_i))
                st(v.tensor_copy(small[:, 2, :], small[:, 1, :]))
                a, b = 2, 3
                d = 1
                while d < BLOCKS:
                    st(v.tensor_copy(small[:, b, 0:d], small[:, a, 0:d]), False)
                    st(v.tensor_tensor(small[:, b, d:], small[:, a, d:], small[:, a, 0:BLOCKS - d], ALU.add))
                    a, b, d = b, a, 2 * d
                st(v.tensor_tensor(small[:, 4, :], small[:, a, :], small[:, 1, :], ALU.subtract))
                st(v.tensor_scalar(carry, small[:, 4, :], float(P), None, ALU.mult))
                st(v.tensor_tensor(tile_cmp[:, :, 1:], small[:, 4, 1:].unsqueeze(1).to_broadcast([P, 8, BLOCKS - 1]),
                                   tile_no.unsqueeze(2).to_broadcast([P, 8, BLOCKS - 1]), ALU.is_le))
                st(v.tensor_reduce(tile_blk, tile_cmp[:, :, 1:], AX, ALU.add))
                if k:
                    dve.wait_ge(blocks_written, 16)
                v.tensor_copy(tile_blk_i, tile_blk).then_inc(blocks_ready, 1)

                m0 += CHUNKS
                with dve.Fori(0, CI) as i:
                    st.enter(i, 3 * CU)
                    for t in range(CU):
                        members(key, i, t, m0)
                    for t in range(CU):
                        dve.wait_ge(chunk_summed, i * CU + (m0 + t + 1 + CU))
                        rank3 = rank_t.rearrange("p (c b) -> p c b", b=BLOCKS)
                        st(v.tensor_tensor(rank3, ps[0:EP, t % 3, 0:CB].rearrange("p (c b) -> p c b", b=BLOCKS),
                                           carry[0:EP, :].unsqueeze(1).to_broadcast([EP, CT, BLOCKS]), ALU.add))
                        st(v.tensor_tensor(rank_t, rank_t, member_bf[:, t, :], ALU.mult))
                        dve.sem_inc(go, 1)
                        st(v.tensor_reduce(pos_f[:, bass.ds(i * CU * CT + t * CT, CT)], rank3, AX, ALU.add), False)
                        v.tensor_tensor(carry, carry, ps[:, 3 + t % 3, 0:BLOCKS], ALU.add).then_inc(chunk_ranked, 1)
                        dve.wait_ge(chunk_ranked, i * CU + (k * CHUNKS + t + 1 + 2))
                    st.leave(CI)
                st(v.tensor_copy(key_t, pos_f))
                st(v.tensor_scalar(to_row[key], key_t, 7, None, ALU.arith_shift_right))
                st(v.tensor_scalar(key_t, key_t, P - 1, None, ALU.bitwise_and))
                v.scalar_tensor_tensor(out=to_row[key], in0=key_t, scalar=float(TILES), in1=to_row[key],
                                       op0=ALU.mult, op1=ALU.add).then_inc(records_ready, 1)
                dve.wait_ge(records_ready, k + 1)

            dve.wait_ge(weights_loaded, 16 * 17)
            for into, of in ((bias[:, 3, :], turned_a[:, 3:6, :]), (a_src[:, :], turned_b[:, 0:3, :]),
                             (a_dst[:, :], turned_b[:, 3:6, :]), (mean[:, 0, :], turned_a[:, 0:3, :])):
                st(v.tensor_scalar(into, of[:, 0, :], coef[:, 0:1], None, ALU.mult))
                for n in range(1, COEFS):
                    ins = v.scalar_tensor_tensor(out=into, in0=of[:, n, :], scalar=coef[:, n:n + 1], in1=into, op0=ALU.mult, op1=ALU.add)
                    if n == COEFS - 1:
                        ins.then_inc(gat_mixed, 1)
                    else:
                        st(ins)
            dve.wait_ge(gat_mixed, 4)
            dve.wait_ge(gat_turned, 1)
            st(v.tensor_copy(w_gat[:, :], ps[:, 7, 0:FEAT]))

            def list_back(k, key):
                dve.wait_ge(list_loaded, 16 * (k + 1))
                node = lists[key][:, :, 2]
                st(v.tensor_scalar(other[key][:, :], node, float(P), None, ALU.is_lt))
                st(v.scalar_tensor_tensor(out=node, in0=other[key][:, :], scalar=float(P), in1=node, op0=ALU.mult, op1=ALU.add))
                st(v.tensor_scalar(node, node, float(-P), None, ALU.add))

            def wide(a):
                return a.unsqueeze(2).to_broadcast([P, BLOCKS, FEAT])

            def heads(a):
                return a.rearrange("p b (h c) -> p (b h) c", c=HC)

            def over_heads(a):
                return a.rearrange("p b h -> p (b h)").unsqueeze(2).to_broadcast([P, BLOCKS * HEADS, HC])

            def norm_relu(k, K=K):
                st(v.tensor_reduce(stat[:, 0, :], X[:, :, :], AX, ALU.add))
                st(v.tensor_scalar(stat[:, 0, :], stat[:, 0, :], -1.0 / FEAT, None, ALU.mult))
                st(v.tensor_tensor(H[:, :, :], X[:, :, :], wide(stat[:, 0, :]), ALU.add))
                st(v.tensor_tensor(K, H[:, :, :], H[:, :, :], ALU.mult))
                st(v.tensor_reduce(stat[:, 1, :], K, AX, ALU.add))
                v.tensor_scalar(stat[:, 1, :], stat[:, 1, :], 1.0 / FEAT, LN_EPS, ALU.mult, ALU.add).then_inc(variance, 1)
                dve.wait_ge(root, k + 1)
                st(v.reciprocal(stat[:, 3, :], stat[:, 2, :]))
                st(v.tensor_tensor(H[:, :, :], H[:, :, :], wide(stat[:, 3, :]), ALU.mult))

            def relu_to_table():
                v.tensor_scalar(H[:, :, :], H[:, :, :], 0.0, None, ALU.max).then_inc(table_ready, 1)

            def block_sums(name, width=FEAT, weights=None, aux=None, scale_by_weight=False):
                key = name[-1]
                n0, g0, a0 = tiles_before(PASSES, name), tiles_before(GATHERED, name), tiles_before(ACCUMULATED, name)
                with dve.Fori(0, ITERS) as i:
                    st.enter(i, (1 if weights == "attr" else 0) + (UNROLL if aux else 0))
                    blk = blocks_of_body(mybir.EngineType.DVE, key, i)
                    if weights == "attr":
                        st(v.tensor_tensor(share16[:, :, :], lists[key][:, bass.ds(i * UNROLL, UNROLL), 3:3 + HEADS],
                                           other[key][:, bass.ds(i * UNROLL, UNROLL)].unsqueeze(2).to_broadcast([P, UNROLL, HEADS]), ALU.mult))
                    for s in range(UNROLL + 2):
                        if s < UNROLL:
                            dve.wait_ge(summed, i * UNROLL + (n0 + s + UNROLL - RING + 1))
                            node = lists[key][:, bass.ds(i * UNROLL + s, 1), 2]
                            if scale_by_weight:
                                v.tensor_scalar(onehot[:, s % RING, :], iota[:, :], node, lists[key][:, bass.ds(i * UNROLL + s, 1), 7],
                                                ALU.is_equal, ALU.mult).then_inc(tile_members, 1)
                            else:
                                v.tensor_scalar(onehot[:, s % RING, :], iota[:, :], node, None, ALU.is_equal).then_inc(tile_members, 1)
                            if weights:
                                dve.wait_ge(landed[s], i * 16 + (g0 // UNROLL * 16 + 16))
                                w = share16[:, s, :] if weights == "attr" else share[:, bass.ds(i * UNROLL + s, 1), :].rearrange("p t h -> p (t h)")
                                if aux:
                                    a = lists[key][:, bass.ds(i * UNROLL + s, 1), 3:3 + HEADS] if aux == "attr" else share[:, bass.ds(i * UNROLL + s, 1), :]
                                    st(move(scaled[:, s % RING, FEAT:AUX], a.rearrange("p t h -> p (t h)")), False)
                                v.tensor_tensor(scaled[:, s % RING, 0:FEAT].rearrange("p (h c) -> p h c", c=HC),
                                                rows[:, s, 0:FEAT].rearrange("p (h c) -> p h c", c=HC),
                                                w.unsqueeze(2).to_broadcast([P, HEADS, HC]), ALU.mult).then_inc(tile_scaled, 1)
                        if s >= 2:
                            q = s - 2
                            dve.wait_ge(summed, i * UNROLL + (n0 + q + UNROLL + 1))
                            dve.wait_ge(added, i * UNROLL + (a0 + q + RING))
                            at = ACC[:, bass.ds(blk[q], 1), 0:width].rearrange("p b f -> p (b f)")
                            v.tensor_tensor(at, at, ps[:, q % RING, 0:width], ALU.add).then_inc(added, 1)
                    st.leave(ITERS)
                dve.wait_ge(added, a0 + TILES + RING)

            def dense(k):
                pair = k < 3
                with dve.Fori(0, GI) as i:
                    st.enter(i, (3 if pair else 1) + (1 if k < 2 else 0))
                    c = 7 * k + 1
                    hold = move(held[:, :, :], H[:, bass.ds(i * GB, GB), :])
                    if pair:
                        st(hold, False)
                        v.tensor_tensor(mean[:, :, :], ACC[:, bass.ds(i * GB, GB), 0:FEAT],
                                        rdeg[:, bass.ds(i * GB, GB)].unsqueeze(2).to_broadcast([P, GB, FEAT]), ALU.mult).then_inc(dense_in, 1)
                    else:
                        hold.then_inc(dense_in, 1)
                    dve.wait_ge(dense_turned, i + c)
                    ins = v.tensor_copy(turned_a[:, :, :].rearrange("p g f -> p (g f)"), ps[:, 0:2, :].rearrange("p k f -> p (k f)")[:, 0:GB * P])
                    if pair:
                        st(ins, False)
                        ins = v.tensor_copy(turned_b[:, :, :].rearrange("p g f -> p (g f)"), ps[:, 2:4, :].rearrange("p k f -> p (k f)")[:, 0:GB * P])
                    ins.then_inc(dense_copied, 1)
                    dve.wait_ge(dense_out, i + c)
                    hv = H[:, bass.ds(i * GB, GB), :]
                    st(v.tensor_tensor(hv, ps[:, 4:6, :].rearrange("p k f -> p (k f)")[:, 0:GB * P].rearrange("p (g f) -> p g f", f=FEAT),
                                       bias[:, k, :].unsqueeze(1).to_broadcast([P, GB, FEAT]), ALU.add))
                    if k < 2:
                        st(v.tensor_scalar(hv, hv, 0.0, None, ALU.max))
                    st.leave(GI)

            dve.wait_ge(x_loaded, 32)
            dve.wait_ge(blocks_written, 32)
            norm_relu(0, ACC[:, :, 0:FEAT])
            relu_to_table()
            list_back(0, "F")
            dve.wait_ge(blocks_loaded, 32)
            for k in range(3):
                st(v.memset(ACC, 0.0))
                block_sums(f"sage{k} F", width=AUX if k == 0 else FEAT)
                if k == 0:
                    st(v.tensor_scalar(rdeg[:, :], ACC[:, :, FEAT], 1.0, None, ALU.max))
                    st(v.reciprocal(rdeg[:, :], rdeg[:, :]))
                dve.wait_ge(table_written, 16 * (k + 1))
                dense(k)
                if k < 2:
                    v.memset(peak_tile[:, :], 0.0).then_inc(table_ready, 1)
            st(v.tensor_tensor(X[:, :, :], X[:, :, :], H[:, :, :], ALU.add))

            norm_relu(1)
            st(v.tensor_scalar(H[:, :, :], H[:, :, :], 0.0, None, ALU.max))
            dense(3)
            for vec, into in ((a_src, PEAK[:, :, :]), (a_dst, ADM[:, :, 0:HEADS])):
                st(v.tensor_tensor(K, H[:, :, :], vec[:, :].unsqueeze(1).to_broadcast([P, BLOCKS, FEAT]), ALU.mult))
                st(v.tensor_reduce(into, K.rearrange("p b (h c) -> p b h c", c=HC), AX, ALU.add))
            v.memset(peak_tile[:, 0:1], 0.0).then_inc(table_ready, 1)
            v.memset(peak_tile[:, 1:2], 0.0).then_inc(table_ready, 1)
            dve.wait_ge(table_ready, 5)
            st(v.memset(ADM[:, :, HEADS:], -BIG))
            v.tensor_scalar(never, ident[:, :], -BIG, None, ALU.mult).then_inc(peak_consts, 1)
            n0, g0, a0 = tiles_before(PASSES, "peak F"), tiles_before(GATHERED, "peak F"), tiles_before(ACCUMULATED, "peak F")
            with dve.Fori(0, ITERS) as i:
                st.enter(i, 4 * UNROLL)
                blk = blocks_of_body(mybir.EngineType.DVE, "F", i)
                for s in range(UNROLL + 3):
                    if s < UNROLL:
                        dve.wait_ge(summed, i * UNROLL + (n0 + s + UNROLL - RING + 1))
                        node = lists["F"][:, bass.ds(i * UNROLL + s, 1), 2]
                        dve.wait_ge(landed[s], i * 16 + (g0 // UNROLL * 16 + 16))
                        st(move(share[:, bass.ds(i * UNROLL + s, 1), :].rearrange("p t h -> p (t h)"), rows[:, s, 0:HEADS]), False)
                        st(v.tensor_scalar(onehot[:, s % RING, :], iota[:, :], node, None, ALU.is_equal), False)
                        st(v.tensor_scalar(diag[:, s % RING, HEADS - 1, :], ident[:, :], rows[:, s, HEADS - 1:HEADS], None, ALU.mult), False)
                        v.tensor_scalar(absent[:, s % RING, :], iota_bf[:, :], node, None, ALU.not_equal).then_inc(tile_members, 1)
                    if s >= 3:
                        q = s - 3
                        dve.wait_ge(summed, i * UNROLL + (n0 + q + UNROLL + 1))
                        dve.wait_ge(added, i * UNROLL + (a0 + q + RING))
                        st(v.tensor_reduce(peak_tile[:, :], ps[:, q % RING, :].rearrange("p (h e) -> p h e", h=HEADS), AX, ALU.max))
                        at = ADM[:, bass.ds(blk[q], 1), HEADS:].rearrange("p b h -> p (b h)")
                        v.tensor_tensor(at, at, peak_tile[:, :], ALU.max).then_inc(added, 1)
                st.leave(ITERS)
            dve.wait_ge(added, a0 + TILES + RING)
            dve.wait_ge(table_written, 16 * 5)
            st(v.tensor_tensor(PEAK[:, :, :], ADM[:, :, HEADS:], ADM[:, :, 0:HEADS], ALU.add))
            st(v.scalar_tensor_tensor(out=ADM[:, :, HEADS:], in0=PEAK[:, :, :], scalar=SLOPE, in1=PEAK[:, :, :], op0=ALU.mult, op1=ALU.max))
            n0 = tiles_before(PASSES, "share F")
            with dve.Fori(0, ITERS) as i:
                st.enter(i, 2)
                for g in range(UNROLL // RING):
                    dve.wait_ge(turned, i * (UNROLL // RING) + (g + 1))
                    v.tensor_tensor(onehot4[:, g % 2, :, :], iota[:, :].unsqueeze(1).to_broadcast([P, RING, P]),
                                    lists["F"][:, bass.ds(i * UNROLL + g * RING, RING), 2].unsqueeze(2).to_broadcast([P, RING, P]),
                                    ALU.is_equal).then_inc(tile_members, RING)
                dve.wait_ge(summed, i * UNROLL + (n0 + 2 * UNROLL))
                v.tensor_copy(adm16.rearrange("p t h -> p (t h)"), ps[:, 6, 0:UNROLL * 2 * HEADS]).then_inc(fetch_read, 1)
                dve.wait_ge(fetch_read, i + 2)
                dve.wait_ge(shares_exp, i + 1)
                st(v.tensor_tensor(alpha16[:, 0, :, :], share[:, bass.ds(i * UNROLL, UNROLL), :], adm16[:, :, 0:HEADS], ALU.add))
                st(v.scalar_tensor_tensor(out=alpha16[:, 1, :, :], in0=alpha16[:, 0, :, :], scalar=SLOPE, in1=alpha16[:, 0, :, :], op0=ALU.mult, op1=ALU.max))
                v.tensor_tensor(alpha16[:, 1, :, :], alpha16[:, 1, :, :], adm16[:, :, HEADS:], ALU.subtract).then_inc(shares_raw, 1)
                st.leave(ITERS)
            dve.wait_ge(shares_exp, ITERS + 1)
            st(v.memset(ACC, 0.0))
            block_sums("gat F", width=AUX, weights="share", aux="share")
            st(v.tensor_scalar(REC[:, :, :], ACC[:, :, FEAT:AUX], 1e-16, None, ALU.add))
            st(v.reciprocal(REC[:, :, :], REC[:, :, :]))
            st(v.tensor_copy(H[:, :, :], ACC[:, :, 0:FEAT]))
            st(v.tensor_tensor(heads(H[:, :, :]), heads(H[:, :, :]), over_heads(REC[:, :, :]), ALU.mult))
            st(v.tensor_tensor(X[:, :, :], X[:, :, :], H[:, :, :], ALU.add))

            norm_relu(2)
            relu_to_table()
            dve.wait_ge(table_ready, 6)
            st(v.tensor_tensor(X[:, :, :], X[:, :, :], H[:, :, :], ALU.add))
            for k in range(4):
                if k:
                    dve.wait_ge(table_written, 16 * (6 + k))
                st(v.memset(ACC, 0.0))
                for key in "FR":
                    if k == 0 and key == "R":
                        list_back(1, "R")
                    block_sums(f"rk{k} {key}", width=AUX if k == 0 else FEAT, weights="attr", aux="attr" if k == 0 else None)
                A = ACC[:, :, 0:FEAT]
                if k == 0:
                    st(v.tensor_scalar(REC[:, :, :], ACC[:, :, FEAT:AUX], TINY, None, ALU.max))
                    st(v.reciprocal(REC[:, :, :], REC[:, :, :]))
                for h in range(HEADS):
                    part_of = ACC[:, :, h * HC:(h + 1) * HC]
                    st(v.tensor_tensor(part_of, part_of, REC[:, :, h].unsqueeze(2).to_broadcast([P, BLOCKS, HC]), ALU.mult), h == HEADS - 1)
                st(v.scalar_tensor_tensor(out=X[:, :, :], in0=A, scalar=(0.125, 0.375, 0.375, 0.125)[k], in1=X[:, :, :], op0=ALU.mult, op1=ALU.add))
                if k == 0:
                    st(v.tensor_copy(K, A))
                    v.scalar_tensor_tensor(out=A, in0=A, scalar=1.0 / 3.0, in1=H[:, :, :], op0=ALU.mult, op1=ALU.add).then_inc(table_ready, 1)
                elif k == 1:
                    st(v.scalar_tensor_tensor(out=A, in0=K, scalar=-1.0 / 3.0, in1=A, op0=ALU.mult, op1=ALU.add))
                    st(v.scalar_tensor_tensor(out=K, in0=K, scalar=2.0 / 3.0, in1=A, op0=ALU.mult, op1=ALU.subtract))
                    v.tensor_tensor(A, A, H[:, :, :], ALU.add).then_inc(table_ready, 1)
                elif k == 2:
                    st(v.tensor_tensor(A, A, K, ALU.add))
                    v.tensor_tensor(A, A, H[:, :, :], ALU.add).then_inc(table_ready, 1)

            norm_relu(3)
            v.tensor_scalar(H[:, :, :], H[:, :, :], 0.0, None, ALU.max).then_inc(bases_free, 1)
            dve.wait_ge(bases_free, 1)
            with dve.Fori(0, GI) as i:
                st.enter(i, 0)
                move(held[:, :, :], H[:, bass.ds(i * GB, GB), :]).then_inc(dense_in, 1)
                dve.wait_ge(dense_turned, i + (7 * 4 + 1))
                move(H[:, bass.ds(i * GB, GB), :], ps[:, 0:2, :].rearrange("p k f -> p (k f)")[:, 0:GB * P].rearrange("p (g f) -> p g f", f=P)).then_inc(dense_copied, 1)
                st.leave(GI)
            for g in range(FEAT // 8):
                dve.wait_ge(rel_mixed, g + 1)
                v.tensor_copy(W_REL.rearrange("p (r o) -> p o r", o=FEAT)[:, g * 8:(g + 1) * 8, :],
                              ps[:, 6 + g % 2, :].rearrange("p (o r) -> p o r", r=RELS)).then_inc(rel_copied, 1)
            v.tensor_copy(held[:, 0, :], H[:, 0, :]).then_inc(block_held, 1)
            for u in range(4):
                dve.wait_ge(rel_product, u + 1)
                if u == 3:
                    dve.wait_ge(rel_written[0], 16)
                v.tensor_copy(stage[:, u % 3, :], ps[:, 4 * (u % 2):4 * (u % 2) + 4, :].rearrange("p k f -> p (k f)")).then_inc(rel_staged, 1)
            with dve.Fori(0, (BLOCKS - 1) // 3) as i:
                move(held[:, 0:3, :], H[:, bass.ds(i * 3 + 1, 3), :]).then_inc(block_held, 1)
                for n in range(12):
                    dve.wait_ge(rel_product, i * 12 + (5 + n))
                    dve.wait_ge(rel_written[(n + 1) % 3], i * 64 + 16 * ((4 + n) // 3))
                    v.tensor_copy(stage[:, (n + 1) % 3, :], ps[:, 4 * (n % 2):4 * (n % 2) + 4, :].rearrange("p k f -> p (k f)")).then_inc(rel_staged, 1)
            st(v.memset(ACC, 0.0))
            block_sums("rel F", scale_by_weight=True)
            with dve.Fori(0, GI) as i:
                st.enter(i, 3)
                move(held[:, :, :], H[:, bass.ds(i * GB, GB), :]).then_inc(dense_in, 1)
                dve.wait_ge(dense_out, i + (7 * 4 + 1))
                st(v.tensor_tensor(mean[:, :, :], ps[:, 4:6, :].rearrange("p k f -> p (k f)")[:, 0:GB * P].rearrange("p (g f) -> p g f", f=FEAT),
                                   ACC[:, bass.ds(i * GB, GB), 0:FEAT], ALU.add))
                st(v.tensor_tensor(mean[:, :, :], mean[:, :, :], bias[:, 4, :].unsqueeze(1).to_broadcast([P, GB, FEAT]), ALU.add))
                xv = X[:, bass.ds(i * GB, GB), :]
                st(v.scalar_tensor_tensor(out=xv, in0=mean[:, :, :], scalar=0.0, in1=xv, op0=ALU.max, op1=ALU.add))
                st.leave(GI)
            v.memset(peak_tile[:, :], 0.0).then_inc(result_ready, 1)

        @block.tensor
        def _(pe):
            mm, tr = nc.tensor.matmul, nc.tensor.transpose
            pe.sem_inc(chunk_summed, CU)
            pe.sem_inc(summed, UNROLL)
            pe.sem_inc(turned, 2)
            pe.wait_ge(consts, 4)
            for k in range(2):
                mm(ps[:, 6, 0:CB], ones[0:EP, :], zeros[0:EP, 0:CB], start=True, stop=False)
                with pe.Fori(0, CI) as i:
                    for t in range(CU):
                        pe.wait_ge(chunk_members, i * CU + (2 * k * CHUNKS + t + 1))
                        mm(ps[:, 6, 0:CB], ones[0:EP, :], member_bf[:, t, :], start=False, stop=False, skip_group_check=True).then_inc(chunk_summed, 1)
                mm(ps[:, 6, 0:CB], ones[0:EP, :], zeros[0:EP, 0:CB], start=False, stop=True).then_inc(counts_closed, 1)
                with pe.Fori(0, CI) as i:
                    for t in range(CU):
                        pe.wait_ge(chunk_members, i * CU + ((2 * k + 1) * CHUNKS + t + 1))
                        pe.wait_ge(chunk_ranked, i * CU + (k * CHUNKS + t + 1))
                        rank, total = ps[:, t % 3, 0:CB], ps[:, 3 + t % 3, 0:BLOCKS]
                        mm(rank, earlier[0:EP, :], member_bf[:, t, :], start=True, stop=False)
                        for c in range(CT - 1):
                            rest = CT - 1 - c
                            mm(rank[:, (c + 1) * BLOCKS:].rearrange("p (c b) -> p c b", b=BLOCKS), ones[0:EP, :],
                               member_bf[:, t, c * BLOCKS:(c + 1) * BLOCKS].unsqueeze(1).to_broadcast([EP, rest, BLOCKS]),
                               start=False, stop=False, skip_group_check=True)
                        mm(rank, ones[0:EP, :], zeros[0:EP, 0:CB], start=False, stop=True)
                        for c in range(CT):
                            ins = mm(total, ones[0:EP, :], member_bf[:, t, c * BLOCKS:(c + 1) * BLOCKS], start=(c == 0), stop=(c == CT - 1))
                        ins.then_inc(chunk_summed, 1)

            pe.wait_ge(gat_mixed, 4)
            tr(ps[:, 7, 0:FEAT], mean[:, 0, :], ident[:, :]).then_inc(gat_turned, 1)

            def block_sums(name, width=FEAT, weighted=False):
                n0, g0, a0 = tiles_before(PASSES, name), tiles_before(GATHERED, name), tiles_before(ACCUMULATED, name)
                with pe.Fori(0, ITERS) as i:
                    for s in range(UNROLL):
                        pe.wait_ge(tile_members, i * UNROLL + (n0 + s + 1))
                        pe.wait_ge(added, i * UNROLL + (a0 + s + 1))
                        if weighted:
                            pe.wait_ge(tile_scaled, i * UNROLL + (tiles_before(WEIGHTED, name) + s + 1))
                            right = scaled[:, s % RING, 0:width]
                        else:
                            pe.wait_ge(landed[s], i * 16 + (g0 // UNROLL * 16 + 16))
                            right = rows[:, s, 0:width]
                        mm(ps[:, s % RING, 0:width], onehot[:, s % RING, :], right, start=True, stop=True).then_inc(summed, 1)

            def turn(dst_bank, of, j):
                return tr(ps[:, dst_bank + j // 4, (j % 4) * P:(j % 4 + 1) * P], of, ident[:, :])

            def dense(k):
                pair = k < 3
                with pe.Fori(0, GI) as i:
                    pe.wait_ge(dense_in, i + (7 * k + 1))
                    for j in range(GB):
                        ins = turn(0, held[:, j, :], j)
                        if pair:
                            ins = turn(2, mean[:, j, :], j)
                    ins.then_inc(dense_turned, 1)
                    pe.wait_ge(dense_copied, i + (7 * k + 1))
                    for j in range(GB):
                        o = ps[:, 4 + j // 4, (j % 4) * P:(j % 4 + 1) * P]
                        ins = mm(o, turned_a[:, j, :], w_pair[:, 2 * k, :] if pair else w_gat[:, :], start=True, stop=not pair)
                        if pair:
                            ins = mm(o, turned_b[:, j, :], w_pair[:, 2 * k + 1, :], start=False, stop=True)
                    ins.then_inc(dense_out, 1)

            for k in range(3):
                block_sums(f"sage{k} F", AUX if k == 0 else FEAT)
                dense(k)
            dense(3)
            pe.wait_ge(peak_consts, 1)
            n0, a0 = tiles_before(PASSES, "peak F"), tiles_before(ACCUMULATED, "peak F")
            with pe.Fori(0, ITERS) as i:
                for s in range(UNROLL):
                    o = ps[:, s % RING, :]
                    pe.wait_ge(tile_members, i * UNROLL + (n0 + s + 1))
                    pe.wait_ge(added, i * UNROLL + (a0 + s + 1))
                    mm(o.rearrange("p (h e) -> p h e", h=HEADS), absent[:, s % RING, :],
                       never.unsqueeze(1).to_broadcast([P, HEADS, P]), start=True, stop=False)
                    pe.wait_ge(diag_ready, i * UNROLL * (HEADS - 1) + (HEADS - 1) * (s + 1))
                    mm(o, onehot[:, s % RING, :], diag[:, s % RING, :, :].rearrange("p h e -> p (h e)"), start=False, stop=True).then_inc(summed, 1)
            n0 = tiles_before(PASSES, "share F")
            with pe.Fori(0, ITERS) as i:
                blk = blocks_of_body(mybir.EngineType.PE, "F", i)
                pe.wait_ge(fetch_read, i + 1)
                for g in range(UNROLL // RING + 1):
                    if g < UNROLL // RING:
                        pe.wait_ge(tile_members, i * UNROLL + (n0 + (g + 1) * RING))
                        for t in range(RING):
                            ins = tr(ps[:, 4 + g % 2, t * P:(t + 1) * P], onehot4[:, g % 2, t, :], ident[:, :])
                        ins.then_inc(turned, 1)
                    if g >= 1:
                        pe.wait_ge(turned_copied, i * (UNROLL // RING) + g)
                        for t in range(RING):
                            q = (g - 1) * RING + t
                            ins = mm(ps[:, 6, q * 2 * HEADS:(q + 1) * 2 * HEADS], member4[:, (g - 1) % 2, t, :],
                                     ADM[:, bass.ds(blk[q], 1), :].rearrange("p b h -> p (b h)"), start=True, stop=True)
                        ins.then_inc(summed, RING)
            block_sums("gat F", AUX, True)
            for k in range(4):
                for key in "FR":
                    block_sums(f"rk{k} {key}", AUX if k == 0 else FEAT, True)
            with pe.Fori(0, GI) as i:
                pe.wait_ge(dense_in, i + (7 * 4 + 1))
                pe.wait_ge(dense_copied, i + 7 * 4)
                for j in range(GB):
                    ins = turn(0, held[:, j, :], j)
                ins.then_inc(dense_turned, 1)
            for g in range(FEAT // 8):
                pe.wait_ge(bases_loaded, 16 * (g // 4 + 1))
                if g >= 2:
                    pe.wait_ge(rel_copied, g - 1)
                for o in range(8):
                    ins = mm(ps[:, 6 + g % 2, o * RELS:(o + 1) * RELS], bases_sb[:, :, (g % 4) * 8 + o], w_comp_t[:, :], start=True, stop=True)
                ins.then_inc(rel_mixed, 1)
            pe.wait_ge(dense_copied, 7 * 5)
            pe.wait_ge(rel_copied, FEAT // 8)

            def product(n):
                q = n % 4
                for c in range(4):
                    ins = mm(ps[:, 4 * (n % 2) + c, :], held[:, n // 4, :],
                             W_REL[:, (4 * q + c) * 512:(4 * q + c + 1) * 512], start=True, stop=True)
                ins.then_inc(rel_product, 1)

            pe.wait_ge(block_held, 1)
            for u in range(4):
                if u >= 2:
                    pe.wait_ge(rel_staged, u - 1)
                product(u)
            with pe.Fori(0, (BLOCKS - 1) // 3) as i:
                pe.wait_ge(block_held, i + 2)
                for n in range(12):
                    pe.wait_ge(rel_staged, i * 12 + (3 + n))
                    product(n)
            block_sums("rel F")
            with pe.Fori(0, GI) as i:
                pe.wait_ge(dense_in, i + (7 * 5 + 1))
                for j in range(GB):
                    ins = mm(ps[:, 4 + j // 4, (j % 4) * P:(j % 4 + 1) * P], held[:, j, :],
                             w_loop[:, :], start=True, stop=True)
                ins.then_inc(dense_out, 1)


_INS = ["x", "src", "dst", "edge_attr3_4x1", "edge_type_64", "edge_weight1", "L0_gnn_W_self0", "L0_gnn_W_neigh0", "L0_gnn_b0",
        "L0_gnn_W_self1", "L0_gnn_W_neigh1", "L0_gnn_b1", "L0_gnn_W_self2", "L0_gnn_W_neigh2", "L0_gnn_b2",
        "L1_gnn_coeffs_t", "L1_gnn_lin_weight", "L1_gnn_lin_bias", "L1_gnn_att_src", "L1_gnn_att_dst",
        "L3_gnn_weight", "L3_gnn_w_comp", "L3_gnn_h_bias", "L3_gnn_loop_weight"]


def kernel(**inputs):
    import numpy as _np
    import concourse.bacc as _bacc
    from concourse import mybir as _mybir
    from concourse.bass_utils import run_bass_kernel_spmd as _run

    nc = _bacc.Bacc("TRN2", target_bir_lowering=False, num_devices=1)
    arrays, args = {}, []
    for name in _INS:
        a = _np.ascontiguousarray(inputs[name])
        arrays[f"in_{name}_dram"] = a
        args.append(nc.dram_tensor(f"in_{name}_dram", a.shape, _mybir.dt.from_np(a.dtype), kind="ExternalInput").ap())
    args.append(nc.dram_tensor("out_0_dram", (NODES, FEAT), _mybir.dt.float32, kind="ExternalOutput").ap())
    gnn_kernel(nc, *args)
    r = _run(nc, [arrays], core_ids=[0])
    return r.results[0]["out_0_dram"]
```

```python
from contextlib import ExitStack

import concourse.bass as bass
from concourse import mybir

F32 = mybir.dt.float32
BF16 = mybir.dt.bfloat16
I32 = mybir.dt.int32
ALU = mybir.AluOpType
ACT = mybir.ActivationFunctionType
AX = mybir.AxisListType.X

P = 128
NODES = 6250
FEAT = 128
HEADS = 4
HC = FEAT // HEADS
EDGES = 106250
RELS = 64
BASES = 16
COEFS = 3
BLOCKS = -(-NODES // P)
LAST = NODES - (BLOCKS - 1) * P
ROWS = BLOCKS * P

EP = 125
EC = EDGES // EP
CT = 10
CHUNKS = EC // CT
CU = 5
CI = CHUNKS // CU
CB = CT * BLOCKS
SU = 10
SI = EC // SU

UNROLL = 16
HALF = UNROLL // 2
MAX_TILES = (EDGES + BLOCKS * (P - 1)) // P
TILES = -(-MAX_TILES // UNROLL) * UNROLL
ITERS = TILES // UNROLL
RING = 4
W = 8
AUX = FEAT + HEADS

GB = 7
GI = BLOCKS // GB
BIG = float(2.0 ** 100)
TINY = float(2.0 ** -126)
LN_EPS = 1e-5
SLOPE = 0.2
assert EP * EC == EDGES and CI * CU * CT == EC and SI * SU == EC and GB * GI == BLOCKS
assert TILES % 8 == 0 and TILES // 8 <= P and CB <= 512

PASSES = ["sage0 F", "sage1 F", "sage2 F", "peak F", "share F", "gat F",
          "rk0 F", "rk0 R", "rk1 F", "rk1 R", "rk2 F", "rk2 R", "rk3 F", "rk3 R", "rel F"]
GATHERED = [p for p in PASSES if p != "share F"]
ACCUMULATED = [p for p in PASSES if p not in ("share F",)]
WEIGHTED = [p for p in PASSES if p[:3] in ("gat", "rk0", "rk1", "rk2", "rk3")]
TABLES = ["sage0", "sage1", "sage2", "gat", "rk0", "rk1", "rk2", "rk3"]


PAUSES = {"sage0 F": 9, "sage1 F": 9, "sage2 F": 20, "peak F": 41, "gat F": 6}


def gnn_kernel(nc, x, src, dst, edge_attr, edge_type, edge_weight, W_self0, W_neigh0, b0, W_self1,
               W_neigh1, b1, W_self2, W_neigh2, b2, coeffs, lin_weight, lin_bias, att_src, att_dst,
               rel_weight, w_comp, h_bias, loop_weight, out):
    with ExitStack() as ctx:
        def sb(name, shape, dt=F32):
            return ctx.enter_context(nc.sbuf_tensor(name, shape, dt))

        def sem(name):
            return ctx.enter_context(nc.semaphore(name))

        def dram(name, shape, dt=F32):
            return nc.dram_tensor(name, shape, dt, kind="Internal").ap()

        ctx.enter_context(nc.allow_non_contiguous_dma("rows of single words"))

        table = dram("table", (ROWS, FEAT))
        peak_table = dram("peak_table", (ROWS, HEADS))
        rel_table = dram("rel_table", (ROWS * RELS, FEAT))
        list_dram = {"F": dram("list_f", (P * TILES, W)), "R": dram("list_r", (P * TILES, W))}
        block_dram = {"F": dram("block_f", (TILES,), I32), "R": dram("block_r", (TILES,), I32)}

        X = sb("X", [P, BLOCKS, FEAT])
        H = sb("H", [P, BLOCKS, FEAT])
        work = sb("work", [P, BLOCKS * (FEAT + AUX)])
        K = work[:, 0:BLOCKS * FEAT].rearrange("p (b f) -> p b f", f=FEAT)
        ACC = work[:, BLOCKS * FEAT:].rearrange("p (b f) -> p b f", f=AUX)
        lists = {"F": sb("list_F", [P, TILES, W]), "R": sb("list_R", [P, TILES, W])}
        other = {"F": sb("other_F", [P, TILES]), "R": sb("other_R", [P, TILES])}
        block_of = {"F": sb("block_F", [1, TILES], I32), "R": sb("block_R", [1, TILES], I32)}
        rows = sb("rows", [P, UNROLL, AUX])
        scaled = sb("scaled", [P, RING, AUX])
        onehot = sb("onehot", [P, RING, P])
        index = sb("index", [P, UNROLL], I32)
        record = sb("record", [EP, SU, W])
        target = sb("target", [EP, SU], I32)
        share16 = sb("share16", [P, UNROLL, HEADS])
        iota_i = sb("iota_i", [P, P], I32)
        part_i = sb("part_i", [P, 1], I32)
        iota = sb("iota", [P, P])
        iota_bf = sb("iota_bf", [P, P], BF16)
        part = sb("part", [P, 1])
        ident = sb("ident", [P, P])
        earlier = sb("earlier", [P, P], BF16)
        ones = sb("ones", [P, P], BF16)
        zeros = sb("zeros", [P, 512], BF16)
        w_pair = sb("w_pair", [P, 6, FEAT])
        bias = sb("bias", [P, 5, FEAT])
        a_src = sb("a_src", [P, FEAT])
        a_dst = sb("a_dst", [P, FEAT])
        coef = sb("coef", [P, COEFS])
        w_gat = sb("w_gat", [P, FEAT])
        w_loop = sb("w_loop", [P, FEAT])
        w_comp_t = sb("w_comp_t", [BASES, RELS])
        stat = sb("stat", [P, 4, BLOCKS])
        rdeg = sb("rdeg", [P, BLOCKS])
        PEAK = sb("PEAK", [P, BLOCKS, HEADS])
        ADM = sb("ADM", [P, BLOCKS, 2 * HEADS])
        REC = sb("REC", [P, BLOCKS, HEADS])
        peak_tile = sb("peak_tile", [P, 2, HEADS])
        turned_a = sb("turned_a", [P, GB, P])
        turned_b = sb("turned_b", [P, GB, P])
        mean = sb("mean", [P, GB, P])
        held = rows[:, :, :].rearrange("p s f -> p (s f)")[:, 0:GB * P].rearrange("p (g f) -> p g f", f=P)
        share = work[:, 0:TILES * HEADS].rearrange("p (t h) -> p t h", h=HEADS)
        scratch = work[:, BLOCKS * FEAT:]
        diag = scratch[:, 0:RING * HEADS * P].rearrange("p (s h e) -> p s h e", s=RING, h=HEADS)
        absent = scratch[:, 2048:2048 + RING * P // 2].bitcast(BF16).rearrange("p (s e) -> p s e", s=RING)
        never = scratch[:, 2304:2304 + P // 2].bitcast(BF16)
        node16 = scratch[:, 3600:3600 + UNROLL]
        adm16 = scratch[:, 3200:3200 + UNROLL * 2 * HEADS].rearrange("p (t h) -> p t h", h=2 * HEADS)
        alpha16 = scratch[:, 3400:3400 + 2 * UNROLL * HEADS].rearrange("p (s t h) -> p s t h", s=2, h=HEADS)
        hflat = H[:, :, :].rearrange("p b f -> p (b f)")
        PARTS = 3
        NV = PARTS * 2 * HEADS
        groups_bf = hflat[:, 0:2 * RING * P].bitcast(BF16)
        onehot4 = groups_bf[:, 0:2 * RING * P].rearrange("p (s t e) -> p s t e", s=2, t=RING)
        member4 = groups_bf[:, 2 * RING * P:].rearrange("p (s t e) -> p s t e", s=2, t=RING)
        at = 2 * RING * P
        ADM_PARTS = hflat[:, at:at + BLOCKS * NV // 2].bitcast(BF16).rearrange("p (b k h) -> p b k h", b=BLOCKS, k=PARTS)
        at += BLOCKS * NV // 2
        adm_rest = hflat[:, at:at + BLOCKS * 2 * HEADS].rearrange("p (b h) -> p b h", b=BLOCKS)
        at += BLOCKS * 2 * HEADS
        ident_bf = hflat[:, at:at + P // 2].bitcast(BF16)
        at += P // 2
        parts16 = hflat[:, at:at + UNROLL * NV].rearrange("p (t k h) -> p t k h", k=PARTS, h=2 * HEADS)
        W_REL = work[:, 0:RELS * FEAT]
        SQ = 4 * 512
        stage = lists["R"][:, :, :].rearrange("p t w -> p (t w)")[:, 0:3 * SQ].rearrange("p (s n) -> p s n", s=3)
        bases_sb = work[0:BASES, RELS * FEAT:RELS * FEAT + 4096].rearrange("b (i o) -> b i o", o=32)

        def place(at, n, dt=F32, p=EP):
            v = work[0:p, at:at + n]
            return v if dt == F32 else v.bitcast(dt)

        src_i, dst_i, type_i = (place(EC * k, EC, I32) for k in range(3))
        norm_f = place(EC * 3, EC)
        attr_f = place(EC * 4, EC * HEADS)
        hi_f = {"F": place(EC * 8, EC), "R": place(EC * 9, EC)}
        key_t = place(EC * 10, EC, I32)
        pos_f = place(EC * 11, CU * CT)
        self_f = place(EC * 12, EC)
        key_n = place(3200, CU * CT, I32)
        key_q = place(3200 + CU * CT, CU * CT, I32)
        to_row = {"F": place(0, EC), "R": other["R"][0:EP, 0:EC].bitcast(I32)}
        member_bf = work[0:EP, 900:900 + CU * CB // 2].bitcast(BF16).rearrange("p (s n) -> p s n", s=CU)
        rank_t = work[0:EP, 2200:2200 + CB]
        carry = work[:, 2700:2700 + BLOCKS]
        small = work[:, 2750:2750 + 5 * BLOCKS].rearrange("p (k b) -> p k b", k=5)
        small_i = work[:, 3150:3150 + BLOCKS].bitcast(I32)
        tile_no_i = work[:, 11060:11068].bitcast(I32)
        tile_no = work[:, 11068:11076]
        tile_blk = work[:, 11076:11084]
        tile_blk_i = work[:, 11084:11092].bitcast(I32)
        tile_cmp = work[:, 11100:11100 + 8 * BLOCKS].rearrange("p (t b) -> p t b", b=BLOCKS)

        ps = ctx.enter_context(nc.psum_tensor("ps", [P, 8, 512], F32))

        raw_loaded = sem("raw_loaded")
        weights_loaded = sem("weights_loaded")
        x_loaded = sem("x_loaded")
        iotas = sem("iotas")
        consts = sem("consts")
        pads_ready = sem("pads_ready")
        pads_written = sem("pads_written")
        chunk_members = sem("chunk_members")
        chunk_summed = sem("chunk_summed")
        chunk_ranked = sem("chunk_ranked")
        counts_closed = sem("counts_closed")
        blocks_ready = sem("blocks_ready")
        blocks_written = sem("blocks_written")
        blocks_loaded = sem("blocks_loaded")
        records_ready = sem("records_ready")
        staged = sem("staged")
        pool_staged = sem("pool_staged")
        scattered = [sem(f"scattered{s}") for s in range(SU)]
        list_loaded = sem("list_loaded")
        step = sem("step")
        table_ready = sem("table_ready")
        table_written = sem("table_written")
        variance = sem("variance")
        root = sem("root")
        index_ready = sem("index_ready")
        landed = [sem(f"landed{s}") for s in range(UNROLL)]
        tile_members = sem("tile_members")
        tile_scaled = sem("tile_scaled")
        summed = sem("summed")
        added = sem("added")
        peak_read = sem("peak_read")
        diag_ready = sem("diag_ready")
        turned = sem("turned")
        turned_copied = sem("turned_copied")
        fetched = sem("fetched")
        fetch_read = sem("fetch_read")
        shares_raw = sem("shares_raw")
        shares_exp = sem("shares_exp")
        dense_in = sem("dense_in")
        dense_turned = sem("dense_turned")
        dense_copied = sem("dense_copied")
        dense_out = sem("dense_out")
        gat_mixed = sem("gat_mixed")
        gat_turned = sem("gat_turned")
        layer_ready = sem("layer_ready")
        bases_loaded = sem("bases_loaded")
        bases_free = sem("bases_free")
        rel_mixed = sem("rel_mixed")
        rel_copied = sem("rel_copied")
        rel_product = sem("rel_product")
        rel_staged = sem("rel_staged")
        block_held = sem("block_held")
        rel_written = [sem(f"rel_written{s}") for s in range(3)]
        peak_consts = sem("peak_consts")
        go = sem("go")
        result_ready = sem("result_ready")
        written = sem("written")

        def tiles_before(which, name):
            return TILES * which.index(name)

        def table_at(eng, name):
            eng.wait_ge(table_written, 16 * (TABLES.index(name) + 1 + (TABLES.index(name) >= 3)))

        def blocks_of_body(engine, key, i):
            _, values = nc.values_load_multi_w_load_instructions(
                block_of[key][0:1, bass.ds(i * UNROLL, UNROLL)], engines=(engine,), min_val=0, max_val=BLOCKS - 1,
                skip_runtime_bounds_check_because="each is a count of BLOCKS - 1 comparisons")
            return values

        block = ctx.enter_context(nc.Block())

        @block.sync
        def _(sp):
            for view, arr in ((src_i, src), (dst_i, dst), (type_i, edge_type)):
                sp.dma_start(view, arr.rearrange("(p c) -> p c", p=EP)).then_inc(raw_loaded, 16)
            sp.dma_start(norm_f, edge_weight.rearrange("(p c) o -> p (c o)", p=EP)).then_inc(raw_loaded, 16)
            sp.dma_start(attr_f, edge_attr.rearrange("(p c) h o -> p (c h o)", p=EP)).then_inc(raw_loaded, 16)
            sp.wait_ge(pads_ready, 2)
            for key in "FR":
                sp.dma_start(list_dram[key].rearrange("(p t) w -> p (t w)", p=P),
                             lists[key][:, :, :].rearrange("p t w -> p (t w)")).then_inc(pads_written, 16)
            sp.dma_start(X[:, 0:BLOCKS - 1, :], x[0:(BLOCKS - 1) * P, :].rearrange("(b p) f -> p b f", p=P)).then_inc(x_loaded, 16)
            sp.dma_start(X[0:LAST, BLOCKS - 1, :], x[(BLOCKS - 1) * P:NODES, :]).then_inc(x_loaded, 16)
            for k, key in enumerate("FR"):
                sp.wait_ge(blocks_ready, k + 1)
                sp.dma_start(block_dram[key].rearrange("(p j) -> p j", j=8), tile_blk_i[0:TILES // 8, :]).then_inc(blocks_written, 16)
                sp.wait_ge(blocks_written, 16 * (k + 1))
                sp.dma_start(block_of[key][:, :], block_dram[key].rearrange("(o t) -> o t", o=1)).then_inc(blocks_loaded, 16)
            def load_list(k, key):
                for q in range(SU):
                    sp.wait_ge(scattered[q], 16 * SI * (k + 1))
                sp.dma_start(lists[key][:, :, :].rearrange("p t w -> p (t w)"),
                             list_dram[key].rearrange("(p t) w -> p (t w)", p=P)).then_inc(list_loaded, 16)

            n = 0
            for name in TABLES:
                sp.wait_ge(table_ready, n + 1)
                rows_of = {"rk1": ACC[:, :, 0:FEAT], "rk2": K}.get(name, H[:, :, :])
                sp.dma_start(table.rearrange("(b p) f -> p b f", p=P), rows_of).then_inc(table_written, 16)
                n += 1
                if name == "gat":
                    sp.wait_ge(table_ready, n + 1)
                    sp.dma_start(peak_table.rearrange("(b p) h -> p b h", p=P), PEAK[:, :, :]).then_inc(table_written, 16)
                    n += 1
                if name == "sage0":
                    load_list(0, "F")
                if name == "rk0":
                    load_list(1, "R")
            for q in range(4):
                if q == 0:
                    sp.wait_ge(bases_free, 1)
                else:
                    sp.wait_ge(rel_copied, 4 * q)
                sp.dma_start(bases_sb, rel_weight[:, :, q * 32:(q + 1) * 32]).then_inc(bases_loaded, 16)
            rel_rows = rel_table.rearrange("(b p r) f -> p b (r f)", p=P, r=RELS)
            for q in range(4):
                if q < 3:
                    sp.wait_ge(rel_staged, q + 1)
                    sp.dma_start(rel_rows[:, 0, q * SQ:(q + 1) * SQ], stage[:, q, :]).then_inc(rel_written[q], 16)
            sp.wait_ge(rel_staged, 4)
            sp.dma_start(rel_rows[:, 0, 3 * SQ:], stage[:, 0, :]).then_inc(rel_written[0], 16)
            with sp.Fori(0, (BLOCKS - 1) // 3) as i:
                for n in range(12):
                    sp.wait_ge(rel_staged, i * 12 + (5 + n))
                    sp.dma_start(rel_rows[:, bass.ds(i * 3 + (1 + n // 4), 1), (n % 4) * SQ:(n % 4 + 1) * SQ],
                                 stage[:, (n + 1) % 3, :]).then_inc(rel_written[(n + 1) % 3], 16)
            sp.wait_ge(result_ready, 1)
            sp.dma_start(out[0:(BLOCKS - 1) * P, :].rearrange("(b p) f -> p b f", p=P), X[:, 0:BLOCKS - 1, :]).then_inc(written, 16)
            sp.dma_start(out[(BLOCKS - 1) * P:NODES, :], X[0:LAST, BLOCKS - 1, :]).then_inc(written, 16)
            sp.wait_ge(written, 32)

        @block.gpsimd
        def _(pool):
            nc.gpsimd.iota(iota_i[:, :], pattern=[[1, P]], base=0, channel_multiplier=0).then_inc(iotas, 1)
            nc.gpsimd.iota(part_i[:, :], pattern=[[0, 1]], base=0, channel_multiplier=1).then_inc(iotas, 1)
            nc.gpsimd.iota(tile_no_i, pattern=[[1, 8]], base=0, channel_multiplier=8).then_inc(iotas, 1)
            def scatter_half(key, a):
                for q in range(a, a + SU // 2):
                    pool.indirect_dma_start(out=list_dram[key], out_offset=bass.IndirectOffsetOnAxis(ap=target[:, q:q + 1], axis=0),
                                            in_=record[:, q, :], in_offset=None).then_inc(scattered[q], 16)

            def scatters(i):
                for h in range(2):
                    a = h * SU // 2
                    for q in range(a, a + SU // 2):
                        pool.wait_ge(scattered[q], i * 16 + 16 * SI)
                        pool.sem_inc(go, 1)
                    c = bass.ds(i * SU + a, SU // 2)
                    nc.gpsimd.tensor_copy(target[:, a:a + SU // 2], to_row["R"][:, c]).then_inc(pool_staged, 1)
                    nc.gpsimd.tensor_copy(record[:, a:a + SU // 2, :], lists["R"][0:EP, c, :]).then_inc(pool_staged, 1)
                    pool.wait_ge(pool_staged, i * 4 + 2 * h + 2)
                    pool.sem_inc(go, 1)
                    scatter_half("R", a)

            pool.wait_ge(pads_written, 32)
            with pool.Fori(0, SI) as i:
                for h in range(2):
                    pool.wait_ge(staged, i * 4 + 2 * h + 2)
                    pool.sem_inc(go, 1)
                    scatter_half("F", h * SU // 2)

            def gathers(name, from_table, columns):
                n0 = tiles_before(GATHERED, name)
                m0 = tiles_before(PASSES, name)
                with pool.Fori(0, ITERS) as i:
                    for s in range(UNROLL):
                        if s % HALF == 0:
                            pool.wait_ge(index_ready, i * 2 + (n0 // HALF + s // HALF + 1))
                            pool.sem_inc(go, 1)
                        pool.wait_ge(summed, i * UNROLL + (m0 + s + 1))
                        pool.sem_inc(go, 1)
                        pool.indirect_dma_start(out=rows[:, s, 0:columns], out_offset=None, in_=from_table,
                                                in_offset=bass.IndirectOffsetOnAxis(ap=index[:, s:s + 1], axis=0)).then_inc(landed[s], 16)

            done = 0
            for name in GATHERED:
                stage_name = name.split()[0]
                if stage_name in TABLES:
                    table_at(pool, stage_name)
                    gathers(name, table, FEAT)
                elif stage_name == "peak":
                    pool.wait_ge(table_written, 16 * 5)
                    gathers(name, peak_table, HEADS)
                else:
                    for s in range(3):
                        pool.wait_ge(rel_written[s], 16 * len([n for n in range(4 * BLOCKS) if n % 3 == s]))
                    gathers(name, rel_table, FEAT)
                if name in PAUSES:
                    pool.wait_ge(records_ready, 2 * CI)
                    with pool.Fori(done, done + PAUSES[name]) as i:
                        scatters(i)
                    done += PAUSES[name]
            assert done == SI

        @block.scalar
        def _(act):
            loads = [(w_pair[:, n, :], w) for n, w in enumerate((W_self0, W_neigh0, W_self1, W_neigh1, W_self2, W_neigh2))]
            loads += [(w_loop[:, :], loop_weight), (w_comp_t[:, :], w_comp.rearrange("r b -> b r")),
                      (coef[:, :], coeffs.partition_broadcast(P)), (bias[:, 4, :], h_bias.partition_broadcast(P))]
            loads += [(bias[:, n, :], b.partition_broadcast(P)) for n, b in enumerate((b0, b1, b2))]
            loads += [(turned_a[:, 0:COEFS, :], lin_weight.rearrange("b o i -> o b i")),
                      (turned_a[:, 3:3 + COEFS, :], lin_bias.rearrange("b o -> (b o)").partition_broadcast(P)),
                      (turned_b[:, 0:COEFS, :], att_src.rearrange("b q h c -> (b q h c)").partition_broadcast(P)),
                      (turned_b[:, 3:3 + COEFS, :], att_dst.rearrange("b q h c -> (b q h c)").partition_broadcast(P))]
            for view, arr in loads:
                act.dma_start(view, arr).then_inc(weights_loaded, 16)

            act.sem_inc(shares_exp, 1)
            def indices(name):
                n0 = tiles_before(PASSES, name)
                word = 1 if name == "rel F" else 0
                key = name[-1]
                with act.Fori(0, ITERS) as i:
                    for h in range(2):
                        act.wait_ge(summed, i * UNROLL + (n0 + (h + 1) * HALF))
                        act.sem_inc(go, 1)
                        nc.scalar.copy(index[:, h * HALF:(h + 1) * HALF],
                                       lists[key][:, bass.ds(i * UNROLL + h * HALF, HALF), word]).then_inc(index_ready, 1)

            def root_of(k):
                act.wait_ge(variance, k + 1)
                nc.scalar.sqrt(stat[:, 2, :], stat[:, 1, :]).then_inc(root, 1)

            def peak_pass():
                n0, g0 = tiles_before(PASSES, "peak F"), tiles_before(GATHERED, "peak F")

                def refill(i_from, h):
                    nc.scalar.copy(index[:, h * HALF:(h + 1) * HALF],
                                   lists["F"][:, bass.ds(i_from * UNROLL + UNROLL + h * HALF, HALF), 0]).then_inc(index_ready, 1)

                def diagonals(i, s):
                    act.wait_ge(landed[s], i * 16 + (g0 + 16))
                    act.sem_inc(go, 1)
                    act.wait_ge(summed, i * UNROLL + (n0 + s + UNROLL - RING + 1))
                    act.sem_inc(go, 1)
                    for h in range(HEADS - 1):
                        nc.scalar.mul(diag[:, s % RING, h, :], ident[:, :], rows[:, s, h:h + 1]).then_inc(diag_ready, 1)

                for h in range(2):
                    act.wait_ge(summed, n0 + (h + 1) * HALF)
                    nc.scalar.copy(index[:, h * HALF:(h + 1) * HALF],
                                   lists["F"][:, h * HALF:(h + 1) * HALF, 0]).then_inc(index_ready, 1)
                with act.Fori(0, ITERS - 1) as i:
                    for s in range(UNROLL):
                        diagonals(i, s)
                        if s == HALF - 1:
                            refill(i, 0)
                    refill(i, 1)
                for s in range(UNROLL):
                    diagonals(ITERS - 1, s)

            def share_pass():
                n0 = tiles_before(PASSES, "share F")
                with act.Fori(0, ITERS) as i:
                    for g in range(UNROLL // RING):
                        act.wait_ge(turned, i * (UNROLL // RING) + (g + 3))
                        nc.scalar.copy(member4[:, g % 2, :, :].rearrange("p t e -> p (t e)"), ps[:, 4 + g % 2, :]).then_inc(turned_copied, 1)
                    act.wait_ge(shares_raw, i + 1)
                    act.sem_inc(go, 1)
                    at = share[:, bass.ds(i * UNROLL, UNROLL), :]
                    nc.scalar.activation(at, alpha16[:, 1, :, :], ACT.Exp).then_inc(shares_exp, 1)

            def stage_records(j, u, first=False):
                for h in range(2):
                    a = h * SU // 2
                    if not (first and u == 0):
                        for q in range(a, a + SU // 2):
                            act.wait_ge(scattered[q], 16 * u if first else j * (16 * CU * CT // SU) + 16 * u)
                            if not first:
                                act.sem_inc(go, 1)
                    c = slice(u * SU + a, u * SU + a + SU // 2) if first else bass.ds(j * CU * CT + (u * SU + a), SU // 2)
                    nc.scalar.copy(target[:, a:a + SU // 2], to_row["F"][:, c]).then_inc(staged, 1)
                    nc.scalar.copy(record[:, a:a + SU // 2, :], lists["F"][0:EP, c, :]).then_inc(staged, 1)

            act.wait_ge(records_ready, 1)
            for u in range(CU * CT // SU):
                stage_records(0, u, first=True)
            for start, stop in ((1, 3 * CI // 4), (3 * CI // 4, CI)):
                with act.Fori(start, stop) as j:
                    act.wait_ge(records_ready, j + 1)
                    act.sem_inc(go, 1)
                    for u in range(CU * CT // SU):
                        stage_records(j, u)
                if stop < CI:
                    root_of(0)
            act.wait_ge(list_loaded, 16)
            for name in PASSES:
                if name == "peak F":
                    root_of(1)
                    act.wait_ge(peak_consts, 1)
                    peak_pass()
                elif name == "share F":
                    share_pass()
                else:
                    if name == "rk0 F":
                        root_of(2)
                    if name == "rel F":
                        root_of(3)
                    if name == "rk0 R":
                        act.wait_ge(list_loaded, 32)
                    indices(name)

        class Steps:

            def __init__(self, dve):
                self.dve, self.n, self.reg, self.per = dve, 0, None, 0

            def __call__(self, ins, wait=True):
                self.n += 1
                ins.then_inc(step, 1)
                if wait:
                    self.dve.wait_ge(step, self.n if self.reg is None else self.reg * self.per + (self.n - self.skipped))

            def enter(self, reg, per, start=0):
                self.reg, self.per, self.n0, self.skipped = reg, per, self.n, per * start

            def leave(self, trips):
                assert self.n - self.n0 == self.per, (self.n - self.n0, self.per)
                self.n = self.n0 + self.per * trips
                self.reg = None

        @block.vector
        def _(dve):
            v = nc.vector

            def move(into, of):
                return v.tensor_scalar(into, of, 1.0, None, ALU.mult)

            st = Steps(dve)
            dve.sem_inc(chunk_ranked, 2)
            dve.sem_inc(added, RING)
            dve.sem_inc(fetch_read, 1)

            dve.wait_ge(iotas, 3)
            st(v.tensor_copy(iota[:, :], iota_i[:, :]), False)
            st(v.tensor_copy(iota_bf[:, :], iota_i[:, :]), False)
            st(v.tensor_copy(part[:, :], part_i[:, :]), False)
            st(v.tensor_copy(tile_no, tile_no_i))
            v.tensor_scalar(ident[:, :], iota[:, :], part[:, 0:1], None, ALU.is_equal).then_inc(consts, 1)
            v.tensor_scalar(earlier[:, :], iota[:, :], part[:, 0:1], None, ALU.is_gt).then_inc(consts, 1)
            v.memset(ones[:, :], 1.0).then_inc(consts, 1)
            v.memset(zeros[:, :], 0.0).then_inc(consts, 1)
            st(v.memset(rows[:, :, :], 1.0), False)
            st(v.memset(X[:, BLOCKS - 1, :], 0.0), False)
            for key in "FR":
                st(v.memset(lists[key][:, :, :], 0.0))
                v.memset(lists[key][:, :, 2], -1.0).then_inc(pads_ready, 1)

            dve.wait_ge(raw_loaded, 80)
            dve.wait_ge(pads_written, 32)
            st(v.tensor_tensor(self_f, src_i, dst_i, ALU.is_equal))
            for key, near, far in (("F", dst_i, src_i), ("R", src_i, dst_i)):
                rec = lists[key][0:EP, 0:EC, :]
                st(v.tensor_scalar(key_t, near, 7, None, ALU.arith_shift_right))
                st(v.tensor_copy(hi_f[key], key_t))
                st(v.tensor_scalar(key_t, near, P - 1, None, ALU.bitwise_and))
                st(v.scalar_tensor_tensor(out=rec[:, :, 2], in0=self_f, scalar=float(P), in1=key_t, op0=ALU.mult, op1=ALU.add))
                st(v.tensor_copy(rec[:, :, 0], far))
                st(v.tensor_copy(rec[:, :, 3:3 + HEADS], attr_f.rearrange("p (c h) -> p c h", h=HEADS)))
            rec = lists["F"][0:EP, 0:EC, :]
            st(v.scalar_tensor_tensor(out=rec[:, :, 1], in0=src_i, scalar=float(RELS), in1=type_i, op0=ALU.mult, op1=ALU.add))
            st(v.tensor_copy(rec[:, :, 7], norm_f))

            def members(key, i, t, m0):
                dve.wait_ge(chunk_summed, i * CU + (m0 + t + 1))
                hi = hi_f[key][:, bass.ds(i * CU * CT + t * CT, CT)].unsqueeze(2).to_broadcast([EP, CT, BLOCKS])
                v.tensor_tensor(member_bf[:, t, :].rearrange("p (c b) -> p c b", b=BLOCKS), hi,
                                iota[0:EP, 0:BLOCKS].unsqueeze(1).to_broadcast([EP, CT, BLOCKS]),
                                ALU.is_equal).then_inc(chunk_members, 1)

            for k, key in enumerate("FR"):
                m0 = 2 * k * CHUNKS
                with dve.Fori(0, CI) as i:
                    for t in range(CU):
                        members(key, i, t, m0)
                dve.wait_ge(counts_closed, k + 1)
                st(v.tensor_reduce(small[:, 0, :], ps[:, 6, 0:CB].rearrange("p (c b) -> p b c", b=BLOCKS), AX, ALU.add))
                st(v.tensor_scalar(small_i, small[:, 0, :], float(P - 1), None, ALU.add))
                st(v.tensor_scalar(small_i, small_i, 7, None, ALU.arith_shift_right))
                st(v.tensor_copy(small[:, 1, :], small_i))
                st(v.tensor_copy(small[:, 2, :], small[:, 1, :]))
                a, b = 2, 3
                d = 1
                while d < BLOCKS:
                    st(v.tensor_copy(small[:, b, 0:d], small[:, a, 0:d]), False)
                    st(v.tensor_tensor(small[:, b, d:], small[:, a, d:], small[:, a, 0:BLOCKS - d], ALU.add))
                    a, b, d = b, a, 2 * d
                st(v.tensor_tensor(small[:, 4, :], small[:, a, :], small[:, 1, :], ALU.subtract))
                st(v.tensor_scalar(carry, small[:, 4, :], float(P), None, ALU.mult))
                st(v.tensor_tensor(tile_cmp[:, :, 1:], small[:, 4, 1:].unsqueeze(1).to_broadcast([P, 8, BLOCKS - 1]),
                                   tile_no.unsqueeze(2).to_broadcast([P, 8, BLOCKS - 1]), ALU.is_le))
                st(v.tensor_reduce(tile_blk, tile_cmp[:, :, 1:], AX, ALU.add))
                if k:
                    dve.wait_ge(blocks_written, 16)
                v.tensor_copy(tile_blk_i, tile_blk).then_inc(blocks_ready, 1)

                m0 += CHUNKS
                with dve.Fori(0, CI) as i:
                    st.enter(i, 3 * CU + 3)
                    for t in range(CU):
                        members(key, i, t, m0)
                    for t in range(CU):
                        dve.wait_ge(chunk_summed, i * CU + (m0 + t + 1 + CU))
                        rank3 = rank_t.rearrange("p (c b) -> p c b", b=BLOCKS)
                        st(v.tensor_tensor(rank3, ps[0:EP, t % 3, 0:CB].rearrange("p (c b) -> p c b", b=BLOCKS),
                                           carry[0:EP, :].unsqueeze(1).to_broadcast([EP, CT, BLOCKS]), ALU.add))
                        st(v.tensor_tensor(rank_t, rank_t, member_bf[:, t, :], ALU.mult))
                        st(v.tensor_reduce(pos_f[:, t * CT:(t + 1) * CT], rank3, AX, ALU.add), False)
                        v.tensor_tensor(carry, carry, ps[:, 3 + t % 3, 0:BLOCKS], ALU.add).then_inc(chunk_ranked, 1)
                        dve.wait_ge(chunk_ranked, i * CU + (k * CHUNKS + t + 1 + 2))
                    st(v.tensor_copy(key_n, pos_f))
                    st(v.tensor_scalar(key_q, key_n, 7, None, ALU.arith_shift_right))
                    st(v.tensor_scalar(key_n, key_n, P - 1, None, ALU.bitwise_and))
                    v.scalar_tensor_tensor(out=to_row[key][:, bass.ds(i * CU * CT, CU * CT)], in0=key_n, scalar=float(TILES),
                                           in1=key_q, op0=ALU.mult, op1=ALU.add).then_inc(records_ready, 1)
                    st.leave(CI)
                dve.wait_ge(records_ready, CI * (k + 1))

            dve.wait_ge(weights_loaded, 16 * 17)
            for into, of in ((bias[:, 3, :], turned_a[:, 3:6, :]), (a_src[:, :], turned_b[:, 0:3, :]),
                             (a_dst[:, :], turned_b[:, 3:6, :]), (mean[:, 0, :], turned_a[:, 0:3, :])):
                st(v.tensor_scalar(into, of[:, 0, :], coef[:, 0:1], None, ALU.mult))
                for n in range(1, COEFS):
                    ins = v.scalar_tensor_tensor(out=into, in0=of[:, n, :], scalar=coef[:, n:n + 1], in1=into, op0=ALU.mult, op1=ALU.add)
                    if n == COEFS - 1:
                        ins.then_inc(gat_mixed, 1)
                    else:
                        st(ins)
            dve.wait_ge(gat_mixed, 4)
            dve.wait_ge(gat_turned, 1)
            st(v.tensor_copy(w_gat[:, :], ps[:, 7, 0:FEAT]))

            def list_back(k, key):
                dve.wait_ge(list_loaded, 16 * (k + 1))
                node = lists[key][:, :, 2]
                st(v.tensor_scalar(other[key][:, :], node, float(P), None, ALU.is_lt))
                st(v.scalar_tensor_tensor(out=node, in0=other[key][:, :], scalar=float(P), in1=node, op0=ALU.mult, op1=ALU.add))
                st(v.tensor_scalar(node, node, float(-P), None, ALU.add))

            def wide(a):
                return a.unsqueeze(2).to_broadcast([P, BLOCKS, FEAT])

            def heads(a):
                return a.rearrange("p b (h c) -> p (b h) c", c=HC)

            def over_heads(a):
                return a.rearrange("p b h -> p (b h)").unsqueeze(2).to_broadcast([P, BLOCKS * HEADS, HC])

            def norm_relu(k, K=K):
                st(v.tensor_reduce(stat[:, 0, :], X[:, :, :], AX, ALU.add))
                st(v.tensor_scalar(stat[:, 0, :], stat[:, 0, :], -1.0 / FEAT, None, ALU.mult))
                st(v.tensor_tensor(H[:, :, :], X[:, :, :], wide(stat[:, 0, :]), ALU.add))
                st(v.tensor_tensor(K, H[:, :, :], H[:, :, :], ALU.mult))
                st(v.tensor_reduce(stat[:, 1, :], K, AX, ALU.add))
                v.tensor_scalar(stat[:, 1, :], stat[:, 1, :], 1.0 / FEAT, LN_EPS, ALU.mult, ALU.add).then_inc(variance, 1)
                dve.wait_ge(root, k + 1)
                st(v.reciprocal(stat[:, 3, :], stat[:, 2, :]))
                return v.scalar_tensor_tensor(out=H[:, :, :], in0=H[:, :, :], scalar=0.0, in1=wide(stat[:, 3, :]), op0=ALU.max, op1=ALU.mult)

            def block_sums(name, width=FEAT, weights=None, aux=None, scale_by_weight=False):
                key = name[-1]
                n0, g0, a0 = tiles_before(PASSES, name), tiles_before(GATHERED, name), tiles_before(ACCUMULATED, name)
                with dve.Fori(0, ITERS) as i:
                    st.enter(i, (1 if weights == "attr" else 0) + (UNROLL if aux else 0))
                    blk = blocks_of_body(mybir.EngineType.DVE, key, i)
                    if weights == "attr":
                        st(v.tensor_tensor(share16[:, :, :], lists[key][:, bass.ds(i * UNROLL, UNROLL), 3:3 + HEADS],
                                           other[key][:, bass.ds(i * UNROLL, UNROLL)].unsqueeze(2).to_broadcast([P, UNROLL, HEADS]), ALU.mult))
                    for s in range(UNROLL + 2):
                        if s < UNROLL:
                            dve.wait_ge(summed, i * UNROLL + (n0 + s + UNROLL - RING + 1))
                            node = lists[key][:, bass.ds(i * UNROLL + s, 1), 2]
                            if scale_by_weight:
                                v.tensor_scalar(onehot[:, s % RING, :], iota[:, :], node, lists[key][:, bass.ds(i * UNROLL + s, 1), 7],
                                                ALU.is_equal, ALU.mult).then_inc(tile_members, 1)
                            else:
                                v.tensor_scalar(onehot[:, s % RING, :], iota[:, :], node, None, ALU.is_equal).then_inc(tile_members, 1)
                            if weights:
                                dve.wait_ge(landed[s], i * 16 + (g0 // UNROLL * 16 + 16))
                                w = share16[:, s, :] if weights == "attr" else share[:, bass.ds(i * UNROLL + s, 1), :].rearrange("p t h -> p (t h)")
                                if aux:
                                    a = lists[key][:, bass.ds(i * UNROLL + s, 1), 3:3 + HEADS] if aux == "attr" else share[:, bass.ds(i * UNROLL + s, 1), :]
                                    st(move(scaled[:, s % RING, FEAT:AUX], a.rearrange("p t h -> p (t h)")), False)
                                v.tensor_tensor(scaled[:, s % RING, 0:FEAT].rearrange("p (h c) -> p h c", c=HC),
                                                rows[:, s, 0:FEAT].rearrange("p (h c) -> p h c", c=HC),
                                                w.unsqueeze(2).to_broadcast([P, HEADS, HC]), ALU.mult).then_inc(tile_scaled, 1)
                        if s >= 2:
                            q = s - 2
                            dve.wait_ge(summed, i * UNROLL + (n0 + q + UNROLL + 1))
                            dve.wait_ge(added, i * UNROLL + (a0 + q + RING))
                            at = ACC[:, bass.ds(blk[q], 1), 0:width].rearrange("p b f -> p (b f)")
                            v.tensor_tensor(at, at, ps[:, q % RING, 0:width], ALU.add).then_inc(added, 1)
                    st.leave(ITERS)
                dve.wait_ge(added, a0 + TILES + RING)

            def dense(k):
                pair = k < 3
                with dve.Fori(0, GI) as i:
                    st.enter(i, (3 if pair else 1) + (1 if k < 2 else 0))
                    c = 7 * k + 1
                    hold = move(held[:, :, :], H[:, bass.ds(i * GB, GB), :])
                    if pair:
                        st(hold, False)
                        v.tensor_tensor(mean[:, :, :], ACC[:, bass.ds(i * GB, GB), 0:FEAT],
                                        rdeg[:, bass.ds(i * GB, GB)].unsqueeze(2).to_broadcast([P, GB, FEAT]), ALU.mult).then_inc(dense_in, 1)
                    else:
                        hold.then_inc(dense_in, 1)
                    dve.wait_ge(dense_turned, i + c)
                    ins = v.tensor_copy(turned_a[:, :, :].rearrange("p g f -> p (g f)"), ps[:, 0:2, :].rearrange("p k f -> p (k f)")[:, 0:GB * P])
                    if pair:
                        st(ins, False)
                        ins = v.tensor_copy(turned_b[:, :, :].rearrange("p g f -> p (g f)"), ps[:, 2:4, :].rearrange("p k f -> p (k f)")[:, 0:GB * P])
                    ins.then_inc(dense_copied, 1)
                    dve.wait_ge(dense_out, i + c)
                    hv = H[:, bass.ds(i * GB, GB), :]
                    st(v.tensor_tensor(hv, ps[:, 4:6, :].rearrange("p k f -> p (k f)")[:, 0:GB * P].rearrange("p (g f) -> p g f", f=FEAT),
                                       bias[:, k, :].unsqueeze(1).to_broadcast([P, GB, FEAT]), ALU.add))
                    if k < 2:
                        st(v.tensor_scalar(hv, hv, 0.0, None, ALU.max))
                    st.leave(GI)

            dve.wait_ge(x_loaded, 32)
            dve.wait_ge(blocks_written, 32)
            norm_relu(0, ACC[:, :, 0:FEAT]).then_inc(table_ready, 1)
            list_back(0, "F")
            dve.wait_ge(blocks_loaded, 32)
            for k in range(3):
                st(v.memset(ACC, 0.0))
                block_sums(f"sage{k} F", width=AUX if k == 0 else FEAT)
                if k == 0:
                    st(v.tensor_scalar(rdeg[:, :], ACC[:, :, FEAT], 1.0, None, ALU.max))
                    st(v.reciprocal(rdeg[:, :], rdeg[:, :]))
                dve.wait_ge(table_written, 16 * (k + 1))
                dense(k)
                if k < 2:
                    v.memset(peak_tile[:, 0, :], 0.0).then_inc(table_ready, 1)
            st(v.tensor_tensor(X[:, :, :], X[:, :, :], H[:, :, :], ALU.add))

            st(norm_relu(1))
            dense(3)
            for vec, into in ((a_src, PEAK[:, :, :]), (a_dst, ADM[:, :, 0:HEADS])):
                st(v.tensor_tensor(K, H[:, :, :], vec[:, :].unsqueeze(1).to_broadcast([P, BLOCKS, FEAT]), ALU.mult))
                st(v.tensor_reduce(into, K.rearrange("p b (h c) -> p b h c", c=HC), AX, ALU.add))
            v.memset(peak_tile[:, 0, 0:1], 0.0).then_inc(table_ready, 1)
            v.memset(peak_tile[:, 0, 1:2], 0.0).then_inc(table_ready, 1)
            dve.wait_ge(table_ready, 5)
            st(v.memset(ADM[:, :, HEADS:], -BIG))
            v.tensor_scalar(never, ident[:, :], -BIG, None, ALU.mult).then_inc(peak_consts, 1)
            n0, g0, a0 = tiles_before(PASSES, "peak F"), tiles_before(GATHERED, "peak F"), tiles_before(ACCUMULATED, "peak F")
            with dve.Fori(0, ITERS) as i:
                st.enter(i, 2 * UNROLL + UNROLL // RING + 1)
                blk = blocks_of_body(mybir.EngineType.DVE, "F", i)
                st(move(node16, lists["F"][:, bass.ds(i * UNROLL, UNROLL), 2]))
                for s in range(UNROLL + 3):
                    if s < UNROLL:
                        if s % RING == 0:
                            for q in range(s, s + RING):
                                dve.wait_ge(landed[q], i * 16 + (g0 // UNROLL * 16 + 16))
                            st(move(share[:, bass.ds(i * UNROLL + s, RING), :], rows[:, s:s + RING, 0:HEADS]), False)
                        dve.wait_ge(summed, i * UNROLL + (n0 + s + UNROLL - RING + 1))
                        st(v.tensor_scalar(onehot[:, s % RING, :], iota[:, :], node16[:, s:s + 1], None, ALU.is_equal), False)
                        st(v.tensor_scalar(diag[:, s % RING, HEADS - 1, :], ident[:, :], rows[:, s, HEADS - 1:HEADS], None, ALU.mult), False)
                        v.tensor_scalar(absent[:, s % RING, :], iota_bf[:, :], node16[:, s:s + 1], None, ALU.not_equal).then_inc(tile_members, 1)
                    if s >= 3:
                        q = s - 3
                        dve.wait_ge(peak_read, i * UNROLL + (q + 1))
                        dve.wait_ge(added, i * UNROLL + (a0 + q + RING))
                        at = ADM[:, bass.ds(blk[q], 1), HEADS:].rearrange("p b h -> p (b h)")
                        v.tensor_tensor(at, at, peak_tile[:, q % 2, :], ALU.max).then_inc(added, 1)
                    if 2 <= s < UNROLL + 2:
                        q = s - 2
                        dve.wait_ge(summed, i * UNROLL + (n0 + q + UNROLL + 1))
                        dve.sem_inc(go, 1)
                        v.tensor_reduce(peak_tile[:, q % 2, :], ps[:, q % RING, :].rearrange("p (h e) -> p h e", h=HEADS), AX, ALU.max).then_inc(peak_read, 1)
                st.leave(ITERS)
            dve.wait_ge(added, a0 + TILES + RING)
            dve.wait_ge(table_written, 16 * 5)
            st(v.tensor_tensor(PEAK[:, :, :], ADM[:, :, HEADS:], ADM[:, :, 0:HEADS], ALU.add))
            st(v.scalar_tensor_tensor(out=ADM[:, :, HEADS:], in0=PEAK[:, :, :], scalar=SLOPE, in1=PEAK[:, :, :], op0=ALU.mult, op1=ALU.max))
            st(v.tensor_copy(ident_bf, ident[:, :]), False)
            st(v.tensor_copy(ADM_PARTS[:, :, 0, :], ADM[:, :, :]))
            st(v.tensor_tensor(adm_rest, ADM[:, :, :], ADM_PARTS[:, :, 0, :], ALU.subtract))
            st(v.tensor_copy(ADM_PARTS[:, :, 1, :], adm_rest))
            st(v.tensor_tensor(adm_rest, adm_rest, ADM_PARTS[:, :, 1, :], ALU.subtract))
            st(v.tensor_copy(ADM_PARTS[:, :, 2, :], adm_rest))
            n0 = tiles_before(PASSES, "share F")

            def members_of(i, groups):
                for g in groups:
                    dve.wait_ge(turned, i * (UNROLL // RING) + (g + 1))
                    v.tensor_tensor(onehot4[:, g % 2, :, :], iota[:, :].unsqueeze(1).to_broadcast([P, RING, P]),
                                    lists["F"][:, bass.ds(i * UNROLL + g * RING, RING), 2].unsqueeze(2).to_broadcast([P, RING, P]),
                                    ALU.is_equal).then_inc(tile_members, RING)

            def exponents(i):
                dve.wait_ge(summed, i * UNROLL + (n0 + 2 * UNROLL))
                v.tensor_copy(parts16.rearrange("p t k h -> p (t k h)"), ps[:, 6, 0:UNROLL * NV]).then_inc(fetch_read, 1)
                dve.wait_ge(fetch_read, i + 2)
                st(v.tensor_tensor(adm16, parts16[:, :, 2, :], parts16[:, :, 1, :], ALU.add))
                st(v.tensor_tensor(adm16, adm16, parts16[:, :, 0, :], ALU.add))
                dve.wait_ge(shares_exp, i + 1)
                st(v.tensor_tensor(alpha16[:, 0, :, :], share[:, bass.ds(i * UNROLL, UNROLL), :], adm16[:, :, 0:HEADS], ALU.add))
                st(v.scalar_tensor_tensor(out=alpha16[:, 1, :, :], in0=alpha16[:, 0, :, :], scalar=SLOPE, in1=alpha16[:, 0, :, :], op0=ALU.mult, op1=ALU.max))
                v.tensor_tensor(alpha16[:, 1, :, :], alpha16[:, 1, :, :], adm16[:, :, HEADS:], ALU.subtract).then_inc(shares_raw, 1)

            members_of(0, range(4))
            with dve.Fori(1, ITERS) as i:
                st.enter(i, 4, 1)
                members_of(i, (0, 1))
                exponents(i - 1)
                members_of(i, (2, 3))
                st.leave(ITERS - 1)
            exponents(ITERS - 1)
            dve.wait_ge(shares_exp, ITERS + 1)
            st(v.memset(ACC, 0.0))
            block_sums("gat F", width=AUX, weights="share", aux="share")
            st(v.tensor_scalar(REC[:, :, :], ACC[:, :, FEAT:AUX], 1e-16, None, ALU.add))
            st(v.reciprocal(REC[:, :, :], REC[:, :, :]))
            st(v.tensor_copy(H[:, :, :], ACC[:, :, 0:FEAT]))
            st(v.tensor_tensor(heads(H[:, :, :]), heads(H[:, :, :]), over_heads(REC[:, :, :]), ALU.mult))
            st(v.tensor_tensor(X[:, :, :], X[:, :, :], H[:, :, :], ALU.add))

            norm_relu(2).then_inc(table_ready, 1)
            dve.wait_ge(table_ready, 6)
            st(v.tensor_tensor(X[:, :, :], X[:, :, :], H[:, :, :], ALU.add))
            for k in range(4):
                if k:
                    dve.wait_ge(table_written, 16 * (6 + k))
                st(v.memset(ACC, 0.0))
                for key in "FR":
                    if k == 0 and key == "R":
                        list_back(1, "R")
                    block_sums(f"rk{k} {key}", width=AUX if k == 0 else FEAT, weights="attr", aux="attr" if k == 0 else None)
                A = ACC[:, :, 0:FEAT]
                if k == 0:
                    st(v.tensor_scalar(REC[:, :, :], ACC[:, :, FEAT:AUX], TINY, None, ALU.max))
                    st(v.reciprocal(REC[:, :, :], REC[:, :, :]))
                slope = K if k == 0 else A
                for h in range(HEADS):
                    st(v.tensor_tensor(slope[:, :, h * HC:(h + 1) * HC], ACC[:, :, h * HC:(h + 1) * HC],
                                       REC[:, :, h].unsqueeze(2).to_broadcast([P, BLOCKS, HC]), ALU.mult), h == HEADS - 1)
                if k == 0:
                    v.scalar_tensor_tensor(out=A, in0=K, scalar=1.0 / 3.0, in1=H[:, :, :], op0=ALU.mult, op1=ALU.add).then_inc(table_ready, 1)
                elif k == 1:
                    v.tensor_tensor(K, K, A, ALU.add).then_inc(table_ready, 1)
                elif k == 2:
                    v.tensor_tensor(H[:, :, :], H[:, :, :], A, ALU.add).then_inc(table_ready, 1)
                st(v.scalar_tensor_tensor(out=X[:, :, :], in0=slope, scalar=(0.125, 0.375, 0.375, 0.125)[k], in1=X[:, :, :], op0=ALU.mult, op1=ALU.add))
                if k == 0:
                    st(v.tensor_tensor(H[:, :, :], H[:, :, :], K, ALU.add))
                    st(v.scalar_tensor_tensor(out=K, in0=K, scalar=-4.0 / 3.0, in1=H[:, :, :], op0=ALU.mult, op1=ALU.add))
                elif k == 1:
                    st(v.tensor_tensor(H[:, :, :], H[:, :, :], A, ALU.subtract))

            norm_relu(3).then_inc(bases_free, 1)
            dve.wait_ge(bases_free, 1)
            with dve.Fori(0, GI) as i:
                st.enter(i, 0)
                move(held[:, :, :], H[:, bass.ds(i * GB, GB), :]).then_inc(dense_in, 1)
                dve.wait_ge(dense_turned, i + (7 * 4 + 1))
                move(H[:, bass.ds(i * GB, GB), :], ps[:, 0:2, :].rearrange("p k f -> p (k f)")[:, 0:GB * P].rearrange("p (g f) -> p g f", f=P)).then_inc(dense_copied, 1)
                st.leave(GI)
            for g in range(FEAT // 8):
                dve.wait_ge(rel_mixed, g + 1)
                v.tensor_copy(W_REL.rearrange("p (r o) -> p o r", o=FEAT)[:, g * 8:(g + 1) * 8, :],
                              ps[:, 6 + g % 2, :].rearrange("p (o r) -> p o r", r=RELS)).then_inc(rel_copied, 1)
            v.tensor_copy(held[:, 3, :], H[:, 0, :]).then_inc(block_held, 1)
            v.tensor_copy(held[:, 0:3, :], H[:, 1:4, :]).then_inc(block_held, 3)
            for u in range(4):
                dve.wait_ge(rel_product, u + 1)
                if u == 3:
                    dve.wait_ge(rel_written[0], 16)
                v.tensor_copy(stage[:, u % 3, :], ps[:, 4 * (u % 2):4 * (u % 2) + 4, :].rearrange("p k f -> p (k f)")).then_inc(rel_staged, 1)

            def three_blocks(i, last):
                for n in range(12):
                    dve.wait_ge(rel_product, i * 12 + (5 + n))
                    dve.wait_ge(rel_written[(n + 1) % 3], i * 64 + 16 * ((4 + n) // 3))
                    v.tensor_copy(stage[:, (n + 1) % 3, :], ps[:, 4 * (n % 2):4 * (n % 2) + 4, :].rearrange("p k f -> p (k f)")).then_inc(rel_staged, 1)
                    if n % 4 == 3 and not last:
                        move(held[:, n // 4, :], H[:, bass.ds(i * 3 + (4 + n // 4), 1), :].rearrange("p b f -> p (b f)")).then_inc(block_held, 1)

            with dve.Fori(0, (BLOCKS - 1) // 3 - 1) as i:
                three_blocks(i, False)
            three_blocks((BLOCKS - 1) // 3 - 1, True)
            st(v.memset(ACC, 0.0))
            block_sums("rel F", scale_by_weight=True)
            with dve.Fori(0, GI) as i:
                st.enter(i, 3)
                move(held[:, :, :], H[:, bass.ds(i * GB, GB), :]).then_inc(dense_in, 1)
                dve.wait_ge(dense_out, i + (7 * 4 + 1))
                st(v.tensor_tensor(mean[:, :, :], ps[:, 4:6, :].rearrange("p k f -> p (k f)")[:, 0:GB * P].rearrange("p (g f) -> p g f", f=FEAT),
                                   ACC[:, bass.ds(i * GB, GB), 0:FEAT], ALU.add))
                st(v.tensor_tensor(mean[:, :, :], mean[:, :, :], bias[:, 4, :].unsqueeze(1).to_broadcast([P, GB, FEAT]), ALU.add))
                xv = X[:, bass.ds(i * GB, GB), :]
                st(v.scalar_tensor_tensor(out=xv, in0=mean[:, :, :], scalar=0.0, in1=xv, op0=ALU.max, op1=ALU.add))
                st.leave(GI)
            v.memset(peak_tile[:, 0, :], 0.0).then_inc(result_ready, 1)

        @block.tensor
        def _(pe):
            mm, tr = nc.tensor.matmul, nc.tensor.transpose
            pe.sem_inc(chunk_summed, CU)
            pe.sem_inc(summed, UNROLL)
            pe.sem_inc(turned, 2)
            pe.wait_ge(consts, 4)
            for k in range(2):
                mm(ps[:, 6, 0:CB], ones[0:EP, :], zeros[0:EP, 0:CB], start=True, stop=False)
                with pe.Fori(0, CI) as i:
                    for t in range(CU):
                        pe.wait_ge(chunk_members, i * CU + (2 * k * CHUNKS + t + 1))
                        mm(ps[:, 6, 0:CB], ones[0:EP, :], member_bf[:, t, :], start=False, stop=False, skip_group_check=True).then_inc(chunk_summed, 1)
                mm(ps[:, 6, 0:CB], ones[0:EP, :], zeros[0:EP, 0:CB], start=False, stop=True).then_inc(counts_closed, 1)
                with pe.Fori(0, CI) as i:
                    for t in range(CU):
                        pe.wait_ge(chunk_members, i * CU + ((2 * k + 1) * CHUNKS + t + 1))
                        pe.wait_ge(chunk_ranked, i * CU + (k * CHUNKS + t + 1))
                        rank, total = ps[:, t % 3, 0:CB], ps[:, 3 + t % 3, 0:BLOCKS]
                        mm(rank, earlier[0:EP, :], member_bf[:, t, :], start=True, stop=False)
                        for c in range(CT - 1):
                            rest = CT - 1 - c
                            mm(rank[:, (c + 1) * BLOCKS:].rearrange("p (c b) -> p c b", b=BLOCKS), ones[0:EP, :],
                               member_bf[:, t, c * BLOCKS:(c + 1) * BLOCKS].unsqueeze(1).to_broadcast([EP, rest, BLOCKS]),
                               start=False, stop=False, skip_group_check=True)
                        mm(rank, ones[0:EP, :], zeros[0:EP, 0:CB], start=False, stop=True)
                        for c in range(CT):
                            ins = mm(total, ones[0:EP, :], member_bf[:, t, c * BLOCKS:(c + 1) * BLOCKS], start=(c == 0), stop=(c == CT - 1))
                        ins.then_inc(chunk_summed, 1)

            pe.wait_ge(gat_mixed, 4)
            tr(ps[:, 7, 0:FEAT], mean[:, 0, :], ident[:, :]).then_inc(gat_turned, 1)

            def block_sums(name, width=FEAT, weighted=False):
                n0, g0, a0 = tiles_before(PASSES, name), tiles_before(GATHERED, name), tiles_before(ACCUMULATED, name)
                with pe.Fori(0, ITERS) as i:
                    for s in range(UNROLL):
                        pe.wait_ge(tile_members, i * UNROLL + (n0 + s + 1))
                        pe.wait_ge(added, i * UNROLL + (a0 + s + 1))
                        if weighted:
                            pe.wait_ge(tile_scaled, i * UNROLL + (tiles_before(WEIGHTED, name) + s + 1))
                            right = scaled[:, s % RING, 0:width]
                        else:
                            pe.wait_ge(landed[s], i * 16 + (g0 // UNROLL * 16 + 16))
                            right = rows[:, s, 0:width]
                        mm(ps[:, s % RING, 0:width], onehot[:, s % RING, :], right, start=True, stop=True).then_inc(summed, 1)

            def turn(dst_bank, of, j):
                return tr(ps[:, dst_bank + j // 4, (j % 4) * P:(j % 4 + 1) * P], of, ident[:, :])

            def dense(k):
                pair = k < 3
                with pe.Fori(0, GI) as i:
                    pe.wait_ge(dense_in, i + (7 * k + 1))
                    for j in range(GB):
                        ins = turn(0, held[:, j, :], j)
                        if pair:
                            ins = turn(2, mean[:, j, :], j)
                    ins.then_inc(dense_turned, 1)
                    pe.wait_ge(dense_copied, i + (7 * k + 1))
                    for j in range(GB):
                        o = ps[:, 4 + j // 4, (j % 4) * P:(j % 4 + 1) * P]
                        ins = mm(o, turned_a[:, j, :], w_pair[:, 2 * k, :] if pair else w_gat[:, :], start=True, stop=not pair)
                        if pair:
                            ins = mm(o, turned_b[:, j, :], w_pair[:, 2 * k + 1, :], start=False, stop=True)
                    ins.then_inc(dense_out, 1)

            for k in range(3):
                block_sums(f"sage{k} F", AUX if k == 0 else FEAT)
                dense(k)
            dense(3)
            pe.wait_ge(peak_consts, 1)
            n0, a0 = tiles_before(PASSES, "peak F"), tiles_before(ACCUMULATED, "peak F")
            with pe.Fori(0, ITERS) as i:
                for s in range(UNROLL):
                    o = ps[:, s % RING, :]
                    pe.wait_ge(tile_members, i * UNROLL + (n0 + s + 1))
                    pe.wait_ge(added, i * UNROLL + (a0 + s + 1))
                    mm(o.rearrange("p (h e) -> p h e", h=HEADS), absent[:, s % RING, :],
                       never.unsqueeze(1).to_broadcast([P, HEADS, P]), start=True, stop=False)
                    pe.wait_ge(diag_ready, i * UNROLL * (HEADS - 1) + (HEADS - 1) * (s + 1))
                    mm(o, onehot[:, s % RING, :], diag[:, s % RING, :, :].rearrange("p h e -> p (h e)"), start=False, stop=True).then_inc(summed, 1)
            n0 = tiles_before(PASSES, "share F")
            with pe.Fori(0, ITERS) as i:
                blk = blocks_of_body(mybir.EngineType.PE, "F", i)
                for g in range(UNROLL // RING + 1):
                    if g < UNROLL // RING:
                        pe.wait_ge(tile_members, i * UNROLL + (n0 + (g + 1) * RING))
                        for t in range(RING):
                            ins = mm(ps[:, 4 + g % 2, t * P:(t + 1) * P], onehot4[:, g % 2, t, :], ident_bf, start=True, stop=True)
                        ins.then_inc(turned, 1)
                    if g >= 1:
                        pe.wait_ge(turned_copied, i * (UNROLL // RING) + g)
                        if g == 1:
                            pe.wait_ge(fetch_read, i + 1)
                        for t in range(RING):
                            q = (g - 1) * RING + t
                            ins = mm(ps[:, 6, q * NV:(q + 1) * NV], member4[:, (g - 1) % 2, t, :],
                                     ADM_PARTS[:, bass.ds(blk[q], 1), :, :].rearrange("p b k h -> p (b k h)"), start=True, stop=True)
                        ins.then_inc(summed, RING)
            block_sums("gat F", AUX, True)
            for k in range(4):
                for key in "FR":
                    block_sums(f"rk{k} {key}", AUX if k == 0 else FEAT, True)
            with pe.Fori(0, GI) as i:
                pe.wait_ge(dense_in, i + (7 * 4 + 1))
                pe.wait_ge(dense_copied, i + 7 * 4)
                for j in range(GB):
                    ins = turn(0, held[:, j, :], j)
                ins.then_inc(dense_turned, 1)
            for g in range(FEAT // 8):
                pe.wait_ge(bases_loaded, 16 * (g // 4 + 1))
                if g >= 2:
                    pe.wait_ge(rel_copied, g - 1)
                for o in range(8):
                    ins = mm(ps[:, 6 + g % 2, o * RELS:(o + 1) * RELS], bases_sb[:, :, (g % 4) * 8 + o], w_comp_t[:, :], start=True, stop=True)
                ins.then_inc(rel_mixed, 1)
            pe.wait_ge(dense_copied, 7 * 5)
            pe.wait_ge(rel_copied, FEAT // 8)

            def product(n, slot):
                q = n % 4
                for c in range(4):
                    ins = mm(ps[:, 4 * (n % 2) + c, :], held[:, slot, :],
                             W_REL[:, (4 * q + c) * 512:(4 * q + c + 1) * 512], start=True, stop=True)
                ins.then_inc(rel_product, 1)

            pe.wait_ge(block_held, 1)
            for u in range(4):
                if u >= 2:
                    pe.wait_ge(rel_staged, u - 1)
                product(u, 3)
            with pe.Fori(0, (BLOCKS - 1) // 3) as i:
                for n in range(12):
                    if n % 4 == 0:
                        pe.wait_ge(block_held, i * 3 + (2 + n // 4))
                    pe.wait_ge(rel_staged, i * 12 + (3 + n))
                    product(n, n // 4)
            block_sums("rel F")
            with pe.Fori(0, GI) as i:
                pe.wait_ge(dense_in, i + (7 * 5 + 1))
                for j in range(GB):
                    ins = mm(ps[:, 4 + j // 4, (j % 4) * P:(j % 4 + 1) * P], held[:, j, :],
                             w_loop[:, :], start=True, stop=True)
                ins.then_inc(dense_out, 1)


_INS = ["x", "src", "dst", "edge_attr3_4x1", "edge_type_64", "edge_weight1", "L0_gnn_W_self0", "L0_gnn_W_neigh0", "L0_gnn_b0",
        "L0_gnn_W_self1", "L0_gnn_W_neigh1", "L0_gnn_b1", "L0_gnn_W_self2", "L0_gnn_W_neigh2", "L0_gnn_b2",
        "L1_gnn_coeffs_t", "L1_gnn_lin_weight", "L1_gnn_lin_bias", "L1_gnn_att_src", "L1_gnn_att_dst",
        "L3_gnn_weight", "L3_gnn_w_comp", "L3_gnn_h_bias", "L3_gnn_loop_weight"]


def kernel(**inputs):
    import numpy as _np
    import concourse.bacc as _bacc
    from concourse import mybir as _mybir
    from concourse.bass_utils import run_bass_kernel_spmd as _run

    nc = _bacc.Bacc("TRN2", target_bir_lowering=False, num_devices=1)
    arrays, args = {}, []
    for name in _INS:
        a = _np.ascontiguousarray(inputs[name])
        arrays[f"in_{name}_dram"] = a
        args.append(nc.dram_tensor(f"in_{name}_dram", a.shape, _mybir.dt.from_np(a.dtype), kind="ExternalInput").ap())
    args.append(nc.dram_tensor("out_0_dram", (NODES, FEAT), _mybir.dt.float32, kind="ExternalOutput").ap())
    gnn_kernel(nc, *args)
    r = _run(nc, [arrays], core_ids=[0])
    return r.results[0]["out_0_dram"]
```
